# Optimizing a Trainium2 kernel written in Bass

```python
import numpy as np
import jax
import jax.numpy as jnp

def _softmax(x, axis=-1):
    return jax.nn.softmax(x, axis=axis)
def _gelu(x):
    return jax.nn.gelu(x, approximate=True)
def _silu(x):
    return jax.nn.silu(x)
def _sigmoid(x):
    return jax.nn.sigmoid(x)
def _layernorm(x, axis=-1, eps=1e-5):
    m = jnp.mean(x, axis=axis, keepdims=True)
    v = jnp.var(x, axis=axis, keepdims=True)
    return (x - m) / jnp.sqrt(v + eps)
def _scatter_add(tgt, idx, src, axis=0):
    return tgt.at[idx].add(src)
def _segment_sum(src, seg, n):
    return jax.ops.segment_sum(src, seg, n)

kernel_name = 'mk_conv_preact_d2_conv_nchw64_05008d'

def setup_inputs(seed: int = 0):
    np.random.seed(seed)
    _w = jnp.asarray
    def _rec_inputs():
        import jax
        import jax.numpy as jnp
        _gk = jax.random.key(seed)
        x = -7.109e-05 + 0.9999 * jax.random.normal(jax.random.fold_in(_gk, 1), (16, 64, 256, 256), jnp.float32)
        return x
    x = _rec_inputs()
    def _L0_conv_setup():
        import jax, jax.numpy as jnp
        import numpy as np
        B, C, H, W, K = (16, 64, 256, 256, 7)
        PAD = K // 2
        HID = C // 4
        key = jax.random.key(seed)
        k_x, k_w1, k_w2 = jax.random.split(key, 3)
        x = jax.random.normal(k_x, (B, C, H, W), dtype=jnp.float32)
        w1 = jax.random.normal(k_w1, (C, HID), dtype=jnp.float32) * (1.0 / np.sqrt(C))
        b1 = jnp.zeros((HID,), dtype=jnp.float32)
        w2 = jax.random.normal(k_w2, (HID, C * K * K), dtype=jnp.float32) * (1.0 / np.sqrt(HID))
        b2 = jnp.zeros((C * K * K,), dtype=jnp.float32)
        return {'x': x, 'w1': w1, 'b1': b1, 'w2': w2, 'b2': b2}
    _L0_conv_all = _L0_conv_setup()
    _L0_conv_in = {k: v for k, v in _L0_conv_all.items() if k in ('w1', 'b1', 'w2', 'b2', )}
    del _L0_conv_all

    def _L1_conv_setup():
        import jax, jax.numpy as jnp
        import numpy as np
        from jax import lax
        C = 64
        K = 7
        HALF = K // 2
        SIGMA_MIN = 0.6
        SIGMA_MAX = 1.2
        _SOBEL_X = jnp.array([[-1.0, 0.0, 1.0], [-2.0, 0.0, 2.0], [-1.0, 0.0, 1.0]], dtype=jnp.float32).reshape(1, 1, 3, 3)
        _SOBEL_Y = jnp.transpose(_SOBEL_X, (0, 1, 3, 2))

        def _depthwise3x3(x, kern):
            B, Cc, H, W = x.shape
            y = lax.conv_general_dilated(x.reshape(B * Cc, 1, H, W), kern, window_strides=(1, 1), padding=((1, 1), (1, 1)), dimension_numbers=('NCHW', 'OIHW', 'NCHW'))
            return y.reshape(B, Cc, H, W)

        def _shift_stack(xp, W_out, axis):
            views = [lax.slice_in_dim(xp, i, i + W_out, axis=axis) for i in range(K)]
            return jnp.stack(views, axis=-1)
        key = jax.random.key(seed)
        x = jax.random.normal(key, (4, C, 256, 256), dtype=jnp.float32)
        return {'x': x}
    _L1_conv_all = _L1_conv_setup()
    _L1_conv_in = {k: v for k, v in _L1_conv_all.items() if k in ()}
    del _L1_conv_all

    return {
        "x": x,
        "L0_conv_w1": _L0_conv_in["w1"],
        "L0_conv_b1": _L0_conv_in["b1"],
        "L0_conv_w2": _L0_conv_in["w2"],
        "L0_conv_b2": _L0_conv_in["b2"],
    }

def reference(x, L0_conv_w1, L0_conv_b1, L0_conv_w2, L0_conv_b2):
    import jax
    import jax.numpy as jnp
    def _L0_conv_ref(x, w1, b1, w2, b2):
        import jax, jax.numpy as jnp
        import numpy as np
        B, C, H, W, K = (16, 64, 256, 256, 7)
        PAD = K // 2
        HID = C // 4
        b, c, h, w = x.shape
        pooled = jnp.mean(x, axis=(2, 3))
        hdn = jax.nn.gelu(pooled @ w1 + b1, approximate=False)
        weights = jax.nn.sigmoid(hdn @ w2 + b2).reshape(b * c, 1, K, K)
        xp = jnp.pad(x, ((0, 0), (0, 0), (PAD, PAD), (PAD, PAD)), mode='reflect')
        xp = xp.reshape(1, b * c, h + 2 * PAD, w + 2 * PAD)
        out = jax.lax.conv_general_dilated(xp, weights, window_strides=(1, 1), padding='VALID', dimension_numbers=('NCHW', 'OIHW', 'NCHW'), feature_group_count=b * c)
        return out.reshape(b, c, h, w)

    def _L1_conv_ref(x):
        import jax, jax.numpy as jnp
        import numpy as np
        from jax import lax
        C = 64
        K = 7
        HALF = K // 2
        SIGMA_MIN = 0.6
        SIGMA_MAX = 1.2
        _SOBEL_X = jnp.array([[-1.0, 0.0, 1.0], [-2.0, 0.0, 2.0], [-1.0, 0.0, 1.0]], dtype=jnp.float32).reshape(1, 1, 3, 3)
        _SOBEL_Y = jnp.transpose(_SOBEL_X, (0, 1, 3, 2))

        def _depthwise3x3(x, kern):
            B, Cc, H, W = x.shape
            y = lax.conv_general_dilated(x.reshape(B * Cc, 1, H, W), kern, window_strides=(1, 1), padding=((1, 1), (1, 1)), dimension_numbers=('NCHW', 'OIHW', 'NCHW'))
            return y.reshape(B, Cc, H, W)

        def _shift_stack(xp, W_out, axis):
            views = [lax.slice_in_dim(xp, i, i + W_out, axis=axis) for i in range(K)]
            return jnp.stack(views, axis=-1)
        B, Cc, H, W = x.shape
        gx = _depthwise3x3(x, _SOBEL_X)
        gy = _depthwise3x3(x, _SOBEL_Y)
        edge = (gx ** 2 + gy ** 2).mean(axis=1, keepdims=True)
        emin = edge.min(axis=(2, 3), keepdims=True)
        emax = edge.max(axis=(2, 3), keepdims=True)
        edge = (edge - emin) / (emax + 1e-06)
        sigma = SIGMA_MIN + (SIGMA_MAX - SIGMA_MIN) * edge
        offs = jnp.arange(-HALF, HALF + 1, dtype=x.dtype)
        g = jnp.exp(-offs ** 2 / (2.0 * sigma[..., None] ** 2))
        g = g / g.sum(axis=-1, keepdims=True)
        xp = jnp.pad(x, ((0, 0), (0, 0), (0, 0), (HALF, HALF)))
        out = (_shift_stack(xp, W, axis=3) * g).sum(axis=-1)
        op = jnp.pad(out, ((0, 0), (0, 0), (HALF, HALF), (0, 0)))
        out = (_shift_stack(op, H, axis=2) * g).sum(axis=-1)
        return out

    def _gn(v, G=32, eps=1e-5):
        B_, C_, H_, W_ = v.shape
        g = v.reshape(B_, G, C_ // G, H_, W_)
        m = jnp.mean(g, axis=(2, 3, 4), keepdims=True)
        s = jnp.var(g, axis=(2, 3, 4), keepdims=True)
        return ((g - m) / jnp.sqrt(s + eps)).reshape(v.shape)

    def _ln_c(v, eps=1e-6):
        m = jnp.mean(v, axis=1, keepdims=True)
        s = jnp.var(v, axis=1, keepdims=True)
        return (v - m) / jnp.sqrt(s + eps)

    def _ln_t(v, eps=1e-5):
        m = jnp.mean(v, axis=-1, keepdims=True)
        s = jnp.var(v, axis=-1, keepdims=True)
        return (v - m) / jnp.sqrt(s + eps)

    def _to_tokens(v):
        B_, C_, H_, W_ = v.shape
        return v.reshape(B_, C_, H_ * W_).transpose(0, 2, 1)
    def _from_tokens(t, like):
        B_, C_, H_, W_ = like.shape
        return t.transpose(0, 2, 1).reshape(B_, C_, H_, W_)

    x = x + _L0_conv_ref(_gn(x), L0_conv_w1, L0_conv_b1, L0_conv_w2, L0_conv_b2)
    x = x + _L1_conv_ref(_gn(x))
    return x


_drawn_inputs = setup_inputs


def setup_inputs(seed=0):
    import zlib

    import numpy as np

    out = dict(_drawn_inputs(seed))
    spreads = {'L0_conv_b1': (0.0, 0.366), 'L0_conv_b2': (0.0, 0.1)}
    factors = {'L0_conv_w1': 64.0}
    for name, (base, spread) in spreads.items():
        noise = np.random.default_rng([zlib.crc32(name.encode()), seed]).standard_normal(out[name].shape)
        drawn = base * np.exp(spread * noise) if base else spread * noise
        out[name] = jnp.asarray(drawn.astype(out[name].dtype))
    for name, factor in factors.items():
        out[name] = (out[name] * factor).astype(out[name].dtype)
    return out
```

```python
from contextlib import ExitStack

import concourse.bass as bass
from concourse import mybir

F32 = mybir.dt.float32
F32R = mybir.dt.float32r
ACT = mybir.ActivationFunctionType
ALU = mybir.AluOpType
AX_X = mybir.AxisListType.XY
RMAX = bass.bass_isa.ReduceOp.max

P = 128
B, C, H, W, K = 16, 64, 256, 256, 7
PAD = K // 2
HALVES = H // P
PAIRS = C // 2
HID = C // 4
ROWP = W + PAD
WIDE = W + 2 * PAD
SLOTS = C * HALVES
Y_LEN = SLOTS * ROWP + 8
VLEN = 264
TAP0 = 127
NQ = 4
NIDX = 13
EPS = 1e-5
SIGMA_MIN, SIGMA_SPAN = 0.6, 0.6
SMOOTH, SMOOTH_NEG, DIFF, DIFF2, BLUR = 0, 1, 2, 3, 4
N_BANDS = 7


def build(nc, x, w2_laid, mlp_laid, bands, out):
    x_img = x.rearrange("b c (t p) w -> b c p t w", p=P)
    out_img = out.rearrange("b c (t p) w -> b c p t w", p=P)
    tap_table = nc.dram_tensor("tap_table", (C, K, VLEN), F32).ap()
    tap_main = bass.AP(tensor=tap_table.tensor, offset=PAD, ap=[[K * VLEN, C], [1, P], [VLEN, K], [1, P]])
    beyond_rows = list(range(-PAD, 0)) + list(range(P, P + PAD))
    tap_beyond = nc.dram_tensor("tap_beyond", (C, len(beyond_rows), K, P), F32).ap()
    tap_rows = [bass.AP(tensor=tap_table.tensor, offset=PAD + r, ap=[[K * VLEN, C], [VLEN, K], [1, P]])
                for r in beyond_rows]

    with ExitStack() as ctx:
        def sb(name, shape, dt=F32):
            return ctx.enter_context(nc.sbuf_tensor(name, shape, dt))

        def bank(name):
            return ctx.enter_context(nc.psum_tensor(name, [P, HALVES, W], F32))

        def sem(name):
            return ctx.enter_context(nc.semaphore(name))

        images = sb("images", [P, Y_LEN])
        x_raw = sb("x_raw", [P, 2, HALVES, WIDE])
        x_stream = sb("x_stream", [P, HALVES, W])
        x_parts = sb("x_parts", [P, HALVES, 2, 2, WIDE], F32R)
        halo = sb("halo", [P, HALVES, 2, 2, WIDE], F32R)
        hankel = sb("hankel", [P, K + 1, P])
        taps = sb("taps", [P, 2, K + 1, P], F32R)
        y_parts = sb("y_parts", [P, 2, HALVES, W + 2], F32R)
        pair_sum = sb("pair_sum", [P, PAD, HALVES, W])
        blurred = sb("blurred", [P, HALVES, W])
        b_parts = sb("b_parts", [P, 2, HALVES, W], F32R)
        result = sb("result", [P, 2, HALVES, W])
        gauss = sb("gauss", [P, PAD + 1, HALVES, W])
        edge = sb("edge", [P, HALVES, W])
        band = sb("band", [P, N_BANDS, 3, P], F32R)
        ones = sb("ones", [P, P])
        x_stats = sb("x_stats", [P, C, 6])
        x_mean = sb("x_mean", [P, PAIRS])
        x_mean_neg = sb("x_mean_neg", [P, PAIRS])
        y_mean = sb("y_mean", [P, PAIRS])
        y_std = sb("y_std", [P, PAIRS])
        minus_half = sb("minus_half", [P, PAIRS])
        s1 = sb("s1", [P, 2, 6])
        agg = sb("agg", [P, 2])
        dev = sb("dev", [P, 2])
        dev2 = sb("dev2", [P, 1])
        moments = sb("moments", [P, 2])
        var1 = sb("var1", [P, 3])
        rstd1 = sb("rstd1", [P, 1])
        extreme = sb("extreme", [P, 2])
        extreme_all = sb("extreme_all", [P, 2])
        scale_e = sb("scale_e", [P, 4])

        ps_conv = bank("ps_conv")
        ps_blur = [bank(f"ps_blur{k}") for k in range(PAD)]
        ps_gx = bank("ps_gx")
        ps_gy = bank("ps_gy")
        ps_small = bank("ps_small").rearrange("p t w -> p (t w)")

        const_in = sem("const_in")
        table_zeroed = sem("table_zeroed")
        stream_in = sem("stream_in")
        x_in = [sem(f"x_in{u}") for u in range(2)]
        hankel_in = [sem(f"hankel_in{j}") for j in range(2)]
        halo_in = [sem(f"halo_in{j}") for j in range(6)]
        mlp_in = sem("mlp_in")
        table_in = sem("table_in")
        beyond_in = [sem(f"beyond_in{j}") for j in range(2)]
        stored = [sem(f"stored{u}") for u in range(2)]
        cleared = sem("cleared")
        constants = sem("constants")
        bands_ready = sem("bands_ready")
        streamed = sem("streamed")
        padded = sem("padded")
        x_high = sem("x_high")
        x_low = sem("x_low")
        taps_high = sem("taps_high")
        taps_low = sem("taps_low")
        conv_done = sem("conv_done")
        x1_out = sem("x1_out")
        bn_done = sem("bn_done")
        agg_done = sem("agg_done")
        chain = sem("chain")
        mean_mm = sem("mean_mm")
        moments_out = sem("moments_out")
        normed = sem("normed")
        y_high = sem("y_high")
        y_low = sem("y_low")
        sobel_mm = sem("sobel_mm")
        squared = sem("squared")
        edge_add = sem("edge_add")
        sums = sem("sums")
        hblur = sem("hblur")
        b_high = sem("b_high")
        b_low = sem("b_low")
        vblur_mm = sem("vblur_mm")
        vblur = sem("vblur")
        residual = sem("residual")
        centre = sem("centre")
        xs = sem("xs")
        xs_mm = sem("xs_mm")
        xs_act = sem("xs_act")
        xs_pow = sem("xs_pow")
        maps = sem("maps")
        maps_exp = sem("maps_exp")
        maps_all = sem("maps_all")
        edge_clear = sem("edge_clear")
        held = {e: sem(f"held_{e}") for e in ("act", "dve", "pool", "sp")}
        CHAIN, HSTEPS, VSTEPS = 9, 7, 6
        XS, XS_MM, XS_ACT, MAPS = 22, 5, 2, 18

        def need(eng, s, value):
            if not isinstance(value, int) or value > 0:
                eng.wait_ge(s, value)

        def alone(wait, engine):
            wait.then_inc(held[engine], 1)

        def slot(i, u, d=0):
            off = i * (2 * HALVES * ROWP) + (u * HALVES * ROWP + PAD + d)
            v = images[:, bass.ds(off, HALVES * ROWP)]
            return v.rearrange("p (t w) -> p t w", t=HALVES)[:, :, 0:W]

        def col(t, i):
            return t[:, bass.ds(i, 1)]

        def batches(eng, one):
            one(0, front=True, back=False, stream=True)
            with eng.Fori(1, B - 1) as k:
                one(k, front=True, back=True, stream=True)
            one(B - 1, front=True, back=True, stream=False)
            one(B, front=False, back=True, stream=False)

        def pairs(eng, k, body):
            with eng.Fori(0, PAIRS - 1) as i:
                body(k * PAIRS + i, i, True)
            body(k * PAIRS + (PAIRS - 1), PAIRS - 1, False)

        mlp_in_sb = pair_sum[:, 1].rearrange("p t w -> p (t w)")
        w1_sb = mlp_in_sb[0:C, 0:P]
        b1_sb = mlp_in_sb[:, P:P + 1]
        mask_sb = mlp_in_sb[:, P + 1:P + 1 + NQ]
        b2_sb = mlp_in_sb[0:C, P + 5:P + 5 + NQ * NIDX]
        w2_sb = hankel[:, 0:K, :].rearrange("p a b -> p (a b)")[:, 0:C * NIDX].rearrange("p (c j) -> p c j", j=NIDX)
        scratch = pair_sum[:, 0].rearrange("p t w -> p (t w)")
        tmp_a, tmp_b, tmp_c, ch_mean, pooled = (scratch[:, j * C:(j + 1) * C] for j in range(5))
        gvar = scratch[:, 5 * C:5 * C + PAIRS]
        x_rstd = scratch[:, 5 * C + PAIRS:6 * C]
        small_v = scratch[:, 6 * C:6 * C + 16]
        tap_w = scratch[0:C, 7 * C:7 * C + NQ * NIDX]
        map_t = blurred
        map_u = pair_sum[:, 2]

        block = ctx.enter_context(nc.Block())

        @block.sync
        def _(sp):
            sp.dma_start(images[:, 0:N_BANDS * 3 * P], bands).then_inc(const_in, 16)
            sp.wait_ge(cleared, 4)
            sp.dma_start(tap_table.rearrange("c k v -> c (k v)"),
                         gauss.ap().rearrange("p a t w -> p (a t w)")[0:C, 0:K * VLEN]).then_inc(table_zeroed, 16)

            def load_stream(s, k, c):
                need(sp, streamed, s)
                src = x_img[bass.ds(k, 1), bass.ds(c, 1)].rearrange("a b p t w -> p (a b t) w")
                sp.dma_start(x_stream[:, :, :], src).then_inc(stream_in, 16)

            def load_x(n, k, i, u):
                need(sp, x_low, 2 * n + u - 1)
                src = x_img[bass.ds(k, 1), bass.ds(i * 2 + u, 1)].rearrange("a b p t w -> p (a b t) w")
                sp.dma_start(x_raw[:, u, :, PAD:PAD + W], src).then_inc(x_in[u], 16)

            def load_hankel(m, c):
                need(sp, taps_low, m)
                ch = bass.ds(c, 1)
                sp.dma_start(hankel[:, 0:K, :], tap_main[ch].rearrange("a p d j -> p (a d) j")
                             ).then_inc(hankel_in[0], 16)
                sp.dma_start(hankel[0:len(beyond_rows) * K, K, :], tap_beyond[ch].rearrange("a e d j -> (a e d) j")
                             ).then_inc(hankel_in[1], 16)

            def load_halo(n):
                sp.wait_ge(x_low, 2 * n + 2)
                need(sp, conv_done, 2 * n)
                j = 0
                for t in range(HALVES):
                    for e in range(2 * PAD):
                        if t == 0:
                            row, part = (PAD - e, 0) if e < PAD else (e - PAD, 1)
                        else:
                            row, part = (P - PAD + e, 0) if e < PAD else (P - 2 - (e - PAD), 1)
                        pitch, run = HALVES * 4 * WIDE, 4 * WIDE - 2 * PAD
                        src = bass.AP(tensor=x_parts, offset=row * pitch + part * 4 * WIDE,
                                      ap=[[pitch, 1], [1, K], [1, run]])
                        dst = halo[e * K:(e + 1) * K, t].rearrange("p a b w -> p (a b w)")[:, 0:run]
                        sp.dma_start(dst.bitcast(F32), src.bitcast(F32)).then_inc(halo_in[j % 6], 16)
                        j += 1

            def store(nb, k, i, u):
                sp.wait_ge(vblur, VSTEPS * (2 * nb + u + 1))
                dst = out_img[bass.ds(k, 1), bass.ds(i * 2 + u, 1)].rearrange("a b p t w -> p (a b t) w")
                sp.dma_start(dst, result[:, u]).then_inc(stored[u], 16)

            def load_mlp(k):
                if isinstance(k, int) and k == 0:
                    sp.wait_ge(cleared, 4)
                else:
                    alone(sp.wait_ge(taps_low, C * k), "sp")
                    need(sp, hblur, (k - 1) * (C * HSTEPS))
                sp.dma_start(hankel[:, 0:K, :].rearrange("p a b -> p (a b)")[:, 0:C * NIDX], w2_laid
                             ).then_inc(mlp_in, 16)
                sp.dma_start(mlp_in_sb[:, 0:P + 5 + NQ * NIDX], mlp_laid).then_inc(mlp_in, 16)

            def write_table(k):
                if isinstance(k, int) and k == 0:
                    sp.wait_ge(table_zeroed, 16)
                sp.wait_ge(xs, XS * (k + 1))
                sp.dma_start(tap_table[:, :, TAP0:TAP0 + K], tap_w[:, 0:K * K].rearrange("p (d j) -> p d j", d=K)
                             ).then_inc(table_in, 16)
                sp.wait_ge(table_in, 16 * (k + 1))
                for e, src in enumerate(tap_rows):
                    sp.dma_start(tap_beyond[:, e], src).then_inc(beyond_in[e % 2], 16)
                for s in beyond_in:
                    sp.wait_ge(s, 48 * (k + 1))

            def batch(k, front, back, stream):
                if front:
                    write_table(k)
                    for u in range(2):
                        load_x(k * PAIRS, k, 0, u)
                    load_hankel(k * C, 0)
                    load_halo(k * PAIRS)

                def body(n, i, ahead):
                    if front:
                        load_hankel(2 * n + 1, i * 2 + 1)
                        if ahead:
                            load_x(n + 1, k, i + 1, 0)
                            load_x(n + 1, k, i + 1, 1)
                    if stream:
                        load_stream(2 * n + C, k + 1, i * 2)
                    if front and ahead:
                        load_hankel(2 * n + 2, i * 2 + 2)
                    if back:
                        store(n - PAIRS, k - 1, i, 0)
                    if stream:
                        load_stream(2 * n + C + 1, k + 1, i * 2 + 1)
                    if back:
                        store(n - PAIRS, k - 1, i, 1)
                    if front and ahead:
                        load_halo(n + 1)
                pairs(sp, k, body)
                if stream:
                    load_mlp(k + 1)

            with sp.Fori(0, C) as c:
                load_stream(c, 0, c)
            load_mlp(0)
            batches(sp, batch)
            for u in range(2):
                sp.wait_ge(stored[u], 16 * B * PAIRS)

        @block.gpsimd
        def _(pool):
            def pair_sums(b, i, u, first=False):
                for d in range(1, PAD + 1):
                    if not first:
                        pool.wait_ge(hblur, (b - 1) * HSTEPS + (4, 6, 7)[d - 1])
                    pool.tensor_tensor(pair_sum[:, d - 1], slot(i, u, -d), slot(i, u, d), ALU.add).then_inc(sums, 1)

            def add_centre(b, u):
                pool.wait_ge(residual, b + 1)
                pool.wait_ge(hblur, HSTEPS * (b + 1))
                pool.tensor_tensor(result[:, u], result[:, u], blurred[:, :, :], ALU.add).then_inc(centre, 1)

            def pad_x(n, u):
                alone(pool.wait_ge(x_in[u], 16 * (n + 1)), "pool")
                pitch = 2 * HALVES * WIDE
                base = u * HALVES * WIDE
                src = bass.AP(tensor=x_raw, offset=base + 2 * PAD, ap=[[pitch, P], [WIDE, 2], [W - 5, 2], [-1, PAD]])
                dst = bass.AP(tensor=x_raw, offset=base, ap=[[pitch, P], [WIDE, 2], [W + PAD, 2], [1, PAD]])
                pool.tensor_copy(dst, src).then_inc(padded, 1)

            def split_taps(m):
                pool.wait_ge(taps_high, m + 1)
                rev = bass.AP(tensor=hankel, offset=P - 1, ap=[[(K + 1) * P, P], [P, K + 1], [-1, P]])
                pool.tensor_tensor(taps[:, 1], rev, taps[:, 0].bitcast(F32), ALU.subtract).then_inc(taps_low, 1)

            def group_stats(n, i, back):
                def step(j, ins):
                    ins.then_inc(chain, 1)
                    wait = pool.wait_ge(chain, CHAIN * n + j)
                    if j == 5:
                        alone(wait, "pool")
                pool.wait_ge(agg_done, n + 1)
                step(1, pool.tensor_tensor(dev[:, 0:1], agg[:, 0:1], col(x_mean, i), ALU.subtract))
                step(2, pool.tensor_tensor(dev2[:, :], dev[:, 0:1], dev[:, 0:1], ALU.mult))
                step(3, pool.tensor_tensor(dev[:, 1:2], dev2[:, :], agg[:, 1:2], ALU.add))
                pool.wait_ge(moments_out, n + 1)
                step(4, pool.tensor_tensor(var1[:, 0:1], moments[:, 0:1], moments[:, 0:1], ALU.mult))
                step(5, pool.tensor_tensor(var1[:, 1:2], moments[:, 1:2], var1[:, 0:1], ALU.subtract))
                step(6, pool.tensor_scalar(var1[:, 2:3], var1[:, 1:2], 0.0, EPS, ALU.max, ALU.add))
                need(pool, normed, 2 * n)
                step(7, pool.tensor_tensor(rstd1[:, :], var1[:, 2:3], minus_half[:, 0:1], ALU.pow))
                if back:
                    pool.wait_ge(residual, 2 * n + 2 - C)
                step(8, pool.tensor_tensor(col(y_mean, i), moments[:, 0:1], col(x_mean, i), ALU.add))
                step(9, pool.tensor_tensor(col(y_std, i), var1[:, 2:3], rstd1[:, :], ALU.mult))

            def split_y(m, i, u):
                pool.wait_ge(y_high, m + 1)
                pool.tensor_tensor(y_parts[:, 1, :, 1:1 + W], slot(i, u), y_parts[:, 0, :, 1:1 + W].bitcast(F32),
                                   ALU.subtract).then_inc(y_low, 1)

            def batch(k, front, back, stream):
                if front:
                    pad_x(k * PAIRS, 0)
                    pad_x(k * PAIRS, 1)
                    split_taps(k * C)
                if back:
                    pool.wait_ge(maps, MAPS * k)
                    if front:
                        pool.wait_ge(table_in, 16 * (k + 1))
                    pair_sums(k * C - C, 0, 0, first=True)

                def body(n, i, ahead):
                    b = 2 * n - C
                    if back:
                        pair_sums(b + 1, i, 1)
                        add_centre(b, 0)
                    if front:
                        if ahead:
                            pad_x(n + 1, 0)
                            pad_x(n + 1, 1)
                        split_taps(2 * n + 1)
                    if back:
                        add_centre(b + 1, 1)
                        if ahead:
                            pair_sums(b + 2, i + 1, 0)
                    if front:
                        if ahead:
                            split_taps(2 * n + 2)
                        group_stats(n, i, back)
                        split_y(2 * n, i, 0)
                        split_y(2 * n + 1, i, 1)
                pairs(pool, k, body)
                if stream:
                    x_power(k + 1)
                if front:
                    alone(pool.wait_ge(maps, MAPS * k + 3), "pool")
                    pool.partition_all_reduce(extreme_all[:, :], extreme[:, :], P, RMAX).then_inc(maps_all, 1)

            def x_power(k):
                pool.wait_ge(xs, XS * k + 14)
                pool.tensor_tensor(x_rstd, gvar, minus_half[:, :], ALU.pow).then_inc(xs_pow, 1)

            pool.memset(minus_half[:, :], -0.5).then_inc(constants, 1)
            pool.memset(ones[:, :], 1.0 / P).then_inc(constants, 1)
            pool.wait_ge(constants, 2)
            x_power(0)
            batches(pool, batch)

        @block.scalar
        def _(act):
            def rebuild_x1(b, i, u):
                need(act, stored[u], (b - u) * 8)
                alone(act.wait_ge(normed, b + 1), "act")
                nc.scalar.activation(result[:, u], slot(i, u), ACT.Identity, bias=col(y_mean, i),
                                     scale=col(y_std, i)).then_inc(residual, 1)

            def round_blurred(b):
                act.wait_ge(hblur, HSTEPS * (b + 1))
                need(act, vblur_mm, 3 * b)
                nc.scalar.activation(b_parts[:, 0], blurred[:, :, :], ACT.Copy).then_inc(b_high, 1)

            def move_x1(m, i, u, back):
                if back:
                    act.wait_ge(hblur, HSTEPS * (m - C + 1))
                    act.wait_ge(residual, m - C + 1)
                alone(act.wait_ge(conv_done, m + 1), "act")
                nc.scalar.activation(slot(i, u), ps_conv[:, :, :], ACT.Identity,
                                     bias=col(x_mean, i)).then_inc(x1_out, 1)

            def round_taps(m):
                for s in hankel_in:
                    act.wait_ge(s, 16 * (m + 1))
                need(act, conv_done, m)
                rev = bass.AP(tensor=hankel, offset=P - 1, ap=[[(K + 1) * P, P], [P, K + 1], [-1, P]])
                nc.scalar.activation(taps[:, 0], rev, ACT.Copy).then_inc(taps_high, 1)

            def round_x(n, i, u):
                need(act, conv_done, 2 * n + u - 1)
                alone(act.wait_ge(padded, 2 * n + u + 1), "act")
                nc.scalar.activation(x_parts[:, :, u, 0], x_raw[:, u], ACT.Identity,
                                     bias=col(x_mean_neg, i)).then_inc(x_high, 1)

            def move_moments(n):
                act.wait_ge(mean_mm, n + 1)
                nc.scalar.activation(moments[:, :], ps_small[:, 0:2], ACT.Copy).then_inc(moments_out, 1)

            def round_y(m, i, u):
                need(act, sobel_mm, 2 * m)
                alone(act.wait_ge(normed, m + 1), "act")
                nc.scalar.activation(y_parts[:, 0, :, 1:1 + W], slot(i, u), ACT.Copy).then_inc(y_high, 1)

            def square(m):
                for j, g in enumerate((ps_gx, ps_gy)):
                    act.wait_ge(sobel_mm, 2 * m + j + 1)
                    nc.scalar.activation(g[:, :, :], g[:, :, :], ACT.Square).then_inc(squared, 1)

            def batch(k, front, back, stream):
                if front:
                    act.wait_ge(xs, XS * k + 5)
                    round_x(k * PAIRS, 0, 0)
                    round_x(k * PAIRS, 0, 1)
                    round_taps(k * C)
                if back:
                    round_blurred(k * C - C)

                def body(n, i, ahead):
                    m, b = 2 * n, 2 * n - C
                    if back:
                        rebuild_x1(b, i, 0)
                    if front:
                        move_x1(m, i, 0, back)
                        round_taps(m + 1)
                        if ahead:
                            round_x(n + 1, i + 1, 0)
                    if back:
                        rebuild_x1(b + 1, i, 1)
                        round_blurred(b + 1)
                    if front:
                        move_x1(m + 1, i, 1, back)
                        if ahead:
                            round_taps(m + 2)
                            round_x(n + 1, i + 1, 1)
                        move_moments(n)
                        round_y(m, i, 0)
                        square(m)
                        round_y(m + 1, i, 1)
                    if back and ahead:
                        round_blurred(b + 2)
                    if front:
                        square(m + 1)
                pairs(act, k, body)
                if stream:
                    weights(k + 1)
                if front:
                    for d in range(1, PAD + 1):
                        if d == 1:
                            act.wait_ge(maps, MAPS * k + 11)
                        nc.scalar.activation(gauss[:, d], map_u, ACT.Exp, scale=-float(d * d)).then_inc(maps_exp, 1)

            def weights(k):
                act.wait_ge(mlp_in, 32 * (k + 1))
                act.wait_ge(xs_mm, XS_MM * k + 4)
                nc.scalar.activation(small_v[:, 1:2], ps_small[:, 130:131], ACT.Gelu,
                                     bias=b1_sb).then_inc(xs_act, 1)
                act.wait_ge(xs, XS * k + 20)
                nc.scalar.activation(tap_w, tap_w, ACT.Sigmoid).then_inc(xs_act, 1)

            act.wait_ge(const_in, 16)
            nc.scalar.activation(band.ap().rearrange("p a b c -> p (a b c)"), images[:, 0:N_BANDS * 3 * P],
                                 ACT.Copy).then_inc(bands_ready, 1)
            weights(0)
            batches(act, batch)

        @block.tensor
        def _(pe):
            def banded(ps, kind, parts, start, stop):
                last = None
                for j, part in enumerate(parts):
                    nc.tensor.matmul(ps[:, :, :], band[:, kind, 0], part, start=start and j == 0, stop=False)
                    nc.tensor.matmul(ps[:, 0], band[:, kind, 1], part[:, 1], start=False, stop=False)
                    last = nc.tensor.matmul(ps[:, 1], band[:, kind, 2], part[:, 0], start=False,
                                            stop=stop and j == len(parts) - 1)
                return last

            def convolve(n, u):
                m = 2 * n + u
                pe.wait_ge(taps_low, m + 1)
                pe.wait_ge(x_low, m + 1)
                need(pe, x1_out, m)
                passes = ((0, 0), (1, 0), (0, 1))
                for j, (tp, xp) in enumerate(passes):
                    for d in range(K):
                        nc.tensor.matmul(ps_conv[:, :, :], taps[:, tp, d], x_parts[:, :, u, xp, d:d + W],
                                         start=(j == 0 and d == 0), stop=False)
                for s in halo_in:
                    pe.wait_ge(s, 32 * (n + 1))
                for j, (tp, xp) in enumerate(passes):
                    last = nc.tensor.matmul(ps_conv[:, :, :], taps[:, tp, K], halo[:, :, u, xp, 0:W],
                                            start=False, stop=(j == 2))
                last.then_inc(conv_done, 1)

            def vertical(b):
                pe.wait_ge(b_low, b + 1)
                need(pe, vblur, b * VSTEPS)
                for d in range(PAD):
                    banded(ps_blur[d], BLUR + d, (b_parts[:, 0], b_parts[:, 1]), True, True).then_inc(vblur_mm, 1)

            def sobel(m):
                pe.wait_ge(y_low, m + 1)
                part = lambda s, hl: y_parts[:, hl, :, 1 + s:1 + s + W]
                need(pe, edge_add, 2 * m)
                banded(ps_gx, SMOOTH, (part(1, 0), part(1, 1)), True, False)
                banded(ps_gx, SMOOTH_NEG, (part(-1, 0), part(-1, 1)), False, True).then_inc(sobel_mm, 1)
                banded(ps_gy, DIFF, (part(1, 0), part(1, 1), part(-1, 0), part(-1, 1)), True, False)
                banded(ps_gy, DIFF2, (part(0, 0), part(0, 1)), False, True).then_inc(sobel_mm, 1)

            def group_mean(n):
                pe.wait_ge(chain, CHAIN * n + 3)
                need(pe, moments_out, n)
                nc.tensor.matmul(ps_small[:, 0:2], ones[:, :], dev[:, :], start=True, stop=True).then_inc(mean_mm, 1)

            def batch(k, front, back, stream):
                def body(n, i, ahead):
                    if front:
                        convolve(n, 0)
                    if back:
                        vertical(2 * n - C)
                    if front:
                        convolve(n, 1)
                        group_mean(n)
                    if back:
                        vertical(2 * n - C + 1)
                    if front:
                        sobel(2 * n)
                        sobel(2 * n + 1)
                pairs(pe, k, body)
                if stream:
                    x_products(k + 1)

            def x_products(k):
                pe.wait_ge(xs, XS * k + 1)
                need(pe, moments_out, k * PAIRS)
                nc.tensor.matmul(ps_small[:, 0:C], ones[:, :], tmp_a, start=True, stop=True).then_inc(xs_mm, 1)
                pe.wait_ge(xs, XS * k + 13)
                nc.tensor.matmul(ps_small[:, C:C + PAIRS], ones[:, :], tmp_c[:, 0:PAIRS], start=True,
                                 stop=True).then_inc(xs_mm, 1)
                pe.wait_ge(xs, XS * k + 17)
                nc.tensor.matmul(ps_small[0:C, 128:129], pooled, ones[:, 0:1], start=True, stop=True)
                nc.tensor.matmul(ps_small[0:C, 129:130], tmp_b, ones[:, 0:1], start=True,
                                 stop=True).then_inc(xs_mm, 1)
                pe.wait_ge(xs, XS * k + 18)
                pe.wait_ge(mlp_in, 32 * (k + 1))
                nc.tensor.matmul(ps_small[:, 130:131], w1_sb, small_v[0:C, 3:4], start=True,
                                 stop=True).then_inc(xs_mm, 1)
                pe.wait_ge(xs, XS * k + 19)
                for j in range(NIDX):
                    last = nc.tensor.matmul(ps_small[0:C, 192 + NQ * j:192 + NQ * (j + 1)], w2_sb[:, :, j],
                                            small_v[:, 8:8 + NQ], start=True, stop=True)
                last.then_inc(xs_mm, 1)

            pe.wait_ge(bands_ready, 1)
            pe.wait_ge(constants, 2)
            pe.wait_ge(cleared, 5)
            x_products(0)
            batches(pe, batch)

        @block.vector
        def _(dve):
            flat = lambda t: t.rearrange("p t w -> p (t w)")

            def horizontal(b, i, u):
                h = HSTEPS * b
                need(dve, centre, b)
                need(dve, b_low, b)
                nc.vector.tensor_tensor(blurred[:, :, :], gauss[:, 0], slot(i, u), ALU.mult).then_inc(hblur, 1)

                def product(d):
                    dve.wait_ge(sums, 3 * b + d)
                    nc.vector.tensor_tensor(pair_sum[:, d - 1], pair_sum[:, d - 1], gauss[:, d],
                                            ALU.mult).then_inc(hblur, 1)

                def add(d, done):
                    dve.wait_ge(hblur, h + done)
                    nc.vector.tensor_tensor(blurred[:, :, :], blurred[:, :, :], pair_sum[:, d - 1],
                                            ALU.add).then_inc(hblur, 1)
                product(1)
                product(2)
                add(1, 2)
                product(3)
                add(2, 4)
                add(3, 6)

            def split_blurred(b):
                dve.wait_ge(b_high, b + 1)
                nc.vector.tensor_tensor(b_parts[:, 1], blurred[:, :, :], b_parts[:, 0].bitcast(F32),
                                        ALU.subtract).then_inc(b_low, 1)

            def vertical(b, u):
                v = VSTEPS * b
                for d in range(PAD):
                    dve.wait_ge(vblur_mm, 3 * b + d + 1)
                    nc.vector.tensor_tensor(ps_blur[d][:, :, :], ps_blur[d][:, :, :], gauss[:, d + 1],
                                            ALU.mult).then_inc(vblur, 1)
                dve.wait_ge(centre, b + 1)
                for d in range(PAD):
                    dve.wait_ge(vblur, v + (1, 4, 5)[d])
                    nc.vector.tensor_tensor(result[:, u], ps_blur[d][:, :, :], result[:, u],
                                            ALU.add).then_inc(vblur, 1)

            def split_x(n, i, u):
                dve.wait_ge(x_high, 2 * n + u + 1)
                nc.vector.scalar_tensor_tensor(
                    out=x_parts[:, :, u, 1], in0=x_raw[:, u], scalar=col(x_mean, i),
                    in1=x_parts[:, :, u, 0].bitcast(F32),
                    op0=ALU.subtract, op1=ALU.subtract).then_inc(x_low, 1)

            def measure_stream(s, c):
                alone(dve.wait_ge(stream_in, 16 * (s + 1)), "dve")
                nc.vector.bn_stats(x_stats[:, bass.ds(c, 1), :].rearrange("p a s -> p (a s)"), flat(x_stream[:, :, :])
                                   ).then_inc(streamed, 1)

            def measure_x1(m, i, u):
                alone(dve.wait_ge(x1_out, m + 1), "dve")
                nc.vector.bn_stats(s1[:, u, :], slot(i, u)).then_inc(bn_done, 1)

            def aggregate(n):
                alone(dve.wait_ge(bn_done, 2 * n + 2), "dve")
                nc.vector.bn_aggr(agg[:, :], s1.ap().rearrange("p u s -> p (u s)")).then_inc(agg_done, 1)

            def norm(n, i, u):
                if u == 0:
                    dve.wait_ge(chain, CHAIN * n + CHAIN)
                nc.vector.tensor_scalar(slot(i, u), slot(i, u), col(y_mean, i), rstd1[:, :], ALU.subtract,
                                        ALU.mult).then_inc(normed, 1)

            def add_edges(m):
                for j, g in enumerate((ps_gx, ps_gy)):
                    dve.wait_ge(squared, 2 * m + j + 1)
                    need(dve, edge_add, 2 * m + j)
                    nc.vector.tensor_tensor(edge[:, :, :], g[:, :, :], edge[:, :, :], ALU.add).then_inc(edge_add, 1)

            def batch(k, front, back, stream):
                if front:
                    nc.vector.memset(edge[:, :, :], 0.0).then_inc(edge_clear, 1)
                    split_x(k * PAIRS, 0, 0)
                    split_x(k * PAIRS, 0, 1)
                    dve.wait_ge(edge_clear, k + 1)
                if back:
                    horizontal(k * C - C, 0, 0)

                def body(n, i, ahead):
                    m, b = 2 * n, 2 * n - C
                    if back:
                        split_blurred(b)
                        horizontal(b + 1, i, 1)
                        split_blurred(b + 1)
                    if front and ahead:
                        split_x(n + 1, i + 1, 0)
                    if back:
                        vertical(b, 0)
                    if stream:
                        measure_stream(m + C, i * 2)
                    if front:
                        measure_x1(m, i, 0)
                        measure_x1(m + 1, i, 1)
                        aggregate(n)
                    if stream:
                        measure_stream(m + C + 1, i * 2 + 1)
                    if front:
                        norm(n, i, 0)
                        norm(n, i, 1)
                    if back:
                        vertical(b + 1, 1)
                    if front and ahead:
                        split_x(n + 1, i + 1, 1)
                    if back and ahead:
                        horizontal(b + 2, i + 1, 0)
                    if front:
                        add_edges(m)
                        add_edges(m + 1)
                pairs(dve, k, body)
                finish(k, front, stream)

            def finish(k, front, stream):
                x, mp = XS * (k + 1), MAPS * k

                if stream:
                    statistics(k + 1, x)
                if front:
                    dve.wait_ge(edge_add, 2 * C * (k + 1))
                    nc.vector.tensor_reduce(extreme[:, 0:1], flat(edge[:, :, :]), mybir.AxisListType.X,
                                            ALU.max).then_inc(maps, 1)
                    nc.vector.tensor_reduce(extreme[:, 1:2], flat(edge[:, :, :]), mybir.AxisListType.X,
                                            ALU.min).then_inc(maps, 1)
                    dve.wait_ge(maps, mp + 2)
                    nc.vector.tensor_scalar(extreme[:, 1:2], extreme[:, 1:2], -1.0, None, ALU.mult).then_inc(maps, 1)
                if stream:
                    hidden_input(k + 1, x)
                if front:
                    dve.wait_ge(maps_all, k + 1)
                    nc.vector.tensor_scalar(scale_e[:, 0:1], extreme_all[:, 0:1], 1.0 / C, 1e-6, ALU.mult,
                                            ALU.add).then_inc(maps, 1)
                    nc.vector.tensor_scalar(scale_e[:, 1:2], extreme_all[:, 1:2], 1.0 / C, None,
                                            ALU.mult).then_inc(maps, 1)
                    dve.wait_ge(maps, mp + 4)
                    nc.vector.reciprocal(scale_e[:, 2:3], scale_e[:, 0:1]).then_inc(maps, 1)
                if stream:
                    hidden_output(k + 1, x)
                if front:
                    dve.wait_ge(maps, mp + 6)
                    need(dve, centre, k * C)
                    nc.vector.tensor_scalar(map_t[:, :, :], edge[:, :, :], 1.0 / C, scale_e[:, 1:2], ALU.mult,
                                            ALU.add).then_inc(maps, 1)
                    dve.wait_ge(maps, mp + 7)
                    nc.vector.tensor_scalar(map_t[:, :, :], map_t[:, :, :], scale_e[:, 2:3], SIGMA_SPAN, ALU.mult,
                                            ALU.mult).then_inc(maps, 1)
                    dve.wait_ge(maps, mp + 8)
                    nc.vector.tensor_scalar(map_u, map_t[:, :, :], SIGMA_MIN, None, ALU.add).then_inc(maps, 1)
                    dve.wait_ge(maps, mp + 9)
                    nc.vector.scalar_tensor_tensor(out=map_t[:, :, :], in0=map_u, scalar=2.0, in1=map_u,
                                                   op0=ALU.mult, op1=ALU.mult).then_inc(maps, 1)
                    dve.wait_ge(maps, mp + 10)
                    nc.vector.reciprocal(map_u, map_t[:, :, :]).then_inc(maps, 1)
                if stream:
                    scale_taps(k + 1, x)
                if front:
                    dve.wait_ge(maps_exp, 3 * (k + 1))
                    nc.vector.tensor_tensor(map_t[:, :, :], gauss[:, 1], gauss[:, 2], ALU.add).then_inc(maps, 1)
                    dve.wait_ge(maps, mp + 12)
                    nc.vector.tensor_tensor(map_t[:, :, :], map_t[:, :, :], gauss[:, 3], ALU.add).then_inc(maps, 1)
                    dve.wait_ge(maps, mp + 13)
                    nc.vector.tensor_scalar(map_t[:, :, :], map_t[:, :, :], 2.0, 1.0, ALU.mult,
                                            ALU.add).then_inc(maps, 1)
                    dve.wait_ge(maps, mp + 14)
                    nc.vector.reciprocal(gauss[:, 0], map_t[:, :, :]).then_inc(maps, 1)
                    dve.wait_ge(maps, mp + 15)
                    for d in range(1, PAD + 1):
                        nc.vector.tensor_tensor(gauss[:, d], gauss[:, d], gauss[:, 0], ALU.mult).then_inc(maps, 1)
                    dve.wait_ge(maps, mp + MAPS)

            def of_pair(t, u):
                return t.rearrange("p (g u) -> p u g", u=2)[:, u]

            def to_channels(t):
                return t.unsqueeze(2).broadcast_to([P, PAIRS, 2])

            def statistics(k, x):
                mean_e, mean_o, m2_e, m2_o = (x_stats[:, :, j] for j in (1, 4, 2, 5))
                groups = lambda t: t.rearrange("p (g u) -> p g u", u=2)
                dve.wait_ge(streamed, C * (k + 1))
                need(dve, hblur, (k - 1) * (C * HSTEPS))
                nc.vector.tensor_tensor(tmp_a, mean_e, mean_o, ALU.add).then_inc(xs, 1)
                dve.wait_ge(xs_mm, XS_MM * k + 1)
                nc.vector.tensor_scalar(ch_mean, ps_small[:, 0:C], 0.5, None, ALU.mult).then_inc(xs, 1)
                dve.wait_ge(xs, x + 2)
                nc.vector.tensor_tensor(tmp_b[:, 0:PAIRS], of_pair(ch_mean, 0), of_pair(ch_mean, 1),
                                        ALU.add).then_inc(xs, 1)
                dve.wait_ge(xs, x + 3)
                need(dve, chain, CHAIN * PAIRS * k)
                nc.vector.tensor_scalar(x_mean[:, :], tmp_b[:, 0:PAIRS], 0.5, None, ALU.mult).then_inc(xs, 1)
                nc.vector.tensor_scalar(x_mean_neg[:, :], tmp_b[:, 0:PAIRS], -0.5, None, ALU.mult).then_inc(xs, 1)
                dve.wait_ge(xs, x + 5)
                mean_b = to_channels(x_mean[:, :])
                nc.vector.tensor_tensor(groups(tmp_a), groups(mean_e), mean_b, ALU.subtract).then_inc(xs, 1)
                nc.vector.tensor_tensor(groups(tmp_b), groups(mean_o), mean_b, ALU.subtract).then_inc(xs, 1)
                dve.wait_ge(xs, x + 7)
                nc.vector.tensor_tensor(tmp_a, tmp_a, tmp_a, ALU.mult).then_inc(xs, 1)
                nc.vector.tensor_tensor(tmp_b, tmp_b, tmp_b, ALU.mult).then_inc(xs, 1)
                dve.wait_ge(xs, x + 9)
                nc.vector.tensor_tensor(tmp_a, tmp_a, tmp_b, ALU.add).then_inc(xs, 1)
                dve.wait_ge(xs, x + 10)
                nc.vector.tensor_tensor(tmp_b, m2_e, m2_o, ALU.add).then_inc(xs, 1)
                dve.wait_ge(xs, x + 11)
                nc.vector.scalar_tensor_tensor(out=tmp_a, in0=tmp_b, scalar=1.0 / W, in1=tmp_a, op0=ALU.mult,
                                               op1=ALU.add).then_inc(xs, 1)
                dve.wait_ge(xs, x + 12)
                nc.vector.tensor_tensor(tmp_c[:, 0:PAIRS], of_pair(tmp_a, 0), of_pair(tmp_a, 1),
                                        ALU.add).then_inc(xs, 1)
                dve.wait_ge(xs_mm, XS_MM * k + 2)
                nc.vector.tensor_scalar(gvar, ps_small[:, C:C + PAIRS], 0.25, EPS, ALU.mult,
                                        ALU.add).then_inc(xs, 1)
                nc.vector.tensor_tensor(groups(pooled), groups(ch_mean), mean_b, ALU.subtract).then_inc(xs, 1)
                dve.wait_ge(xs, x + 15)
                dve.wait_ge(xs_pow, k + 1)
                rstd_b = to_channels(x_rstd)
                nc.vector.tensor_tensor(groups(pooled), groups(pooled), rstd_b, ALU.mult).then_inc(xs, 1)
                nc.vector.tensor_copy(groups(tmp_b), rstd_b).then_inc(xs, 1)

            def hidden_input(k, x):
                dve.wait_ge(xs_mm, XS_MM * k + 3)
                nc.vector.tensor_copy(small_v[0:C, 3:5], ps_small[0:C, 128:130]).then_inc(xs, 1)

            def hidden_output(k, x):
                dve.wait_ge(xs_act, XS_ACT * k + 1)
                nc.vector.tensor_scalar(small_v[:, 8:8 + NQ], mask_sb, small_v[:, 1:2], None,
                                        ALU.mult).then_inc(xs, 1)

            def scale_taps(k, x):
                dve.wait_ge(xs_mm, XS_MM * k + 5)
                nc.vector.tensor_tensor(tap_w, ps_small[0:C, 192:192 + NQ * NIDX], b2_sb, ALU.add).then_inc(xs, 1)
                dve.wait_ge(xs_act, XS_ACT * k + 2)
                nc.vector.tensor_scalar(tap_w, tap_w, small_v[0:C, 4:5], None, ALU.mult).then_inc(xs, 1)
                dve.wait_ge(xs, x + 21)
                mid = PAD * K + PAD
                nc.vector.tensor_scalar(tap_w[:, mid:mid + 1], tap_w[:, mid:mid + 1], 1.0, None,
                                        ALU.add).then_inc(xs, 1)

            nc.vector.memset(gauss[:, :, :, :], 0.0).then_inc(cleared, 1)
            nc.vector.memset(hankel[:, :, :], 0.0).then_inc(cleared, 1)
            nc.vector.memset(halo[:, :, :, :, :].bitcast(F32), 0.0).then_inc(cleared, 1)
            nc.vector.memset(y_parts[:, :, :, :].bitcast(F32), 0.0).then_inc(cleared, 1)
            dve.wait_ge(bands_ready, 1)
            pads = images[:, 0:SLOTS * ROWP].rearrange("p (r w) -> p r w", w=ROWP)
            nc.vector.memset(pads[:, :, 0:PAD], 0.0)
            nc.vector.memset(images[:, SLOTS * ROWP:Y_LEN], 0.0).then_inc(cleared, 1)
            with dve.Fori(0, C) as c:
                measure_stream(c, c)
            dve.wait_ge(cleared, 5)
            statistics(0, 0)
            hidden_input(0, 0)
            hidden_output(0, 0)
            scale_taps(0, 0)
            batches(dve, batch)


def _bands():
    import numpy as np
    rows = np.arange(P)[:, None]
    cols = np.arange(P)[None, :]
    out = np.zeros((P, N_BANDS, 3, P), np.float32)
    for part, dist in enumerate((rows - cols, P + rows - cols, rows - cols - P)):
        smooth = 2.0 * (dist == 0) + (abs(dist) == 1)
        diff = 1.0 * (dist == 1) - (dist == -1)
        kinds = [smooth, -smooth, diff, 2 * diff]
        kinds += [1.0 * (abs(dist) == d) - 2.0 * (dist == 0) for d in range(1, PAD + 1)]
        for kind, m in enumerate(kinds):
            out[:, kind, part] = m
    return out.reshape(P, -1)


def kernel(**inputs):
    import numpy as np
    import concourse.bacc as bacc
    from concourse.bass_utils import run_bass_kernel_spmd

    w1, b1 = np.asarray(inputs["L0_conv_w1"]), np.asarray(inputs["L0_conv_b1"])
    w2, b2 = np.asarray(inputs["L0_conv_w2"]), np.asarray(inputs["L0_conv_b2"])
    w2_taps = w2.reshape(HID, C, K, K).transpose(0, 1, 3, 2).reshape(HID, C, K * K)
    w2_full = np.zeros((HID, C, NQ * NIDX), np.float32)
    w2_full[:, :, :K * K] = w2_taps
    w2_laid = np.zeros((NQ, P // NQ, C, NIDX), np.float32)
    w2_laid[:, :HID] = w2_full.reshape(HID, C, NIDX, NQ).transpose(3, 0, 1, 2)
    mlp = np.zeros((P, P + 5 + NQ * NIDX), np.float32)
    for q in range(NQ):
        at = q * (P // NQ)
        mlp[0:C, at:at + HID] = w1
        mlp[at:at + HID, P] = b1
        mlp[at:at + HID, P + 1 + q] = 1.0
    mlp[0:C, P + 5:P + 5 + K * K] = b2.reshape(C, K, K).transpose(0, 2, 1).reshape(C, K * K)

    arrays = {
        "in_x": np.ascontiguousarray(inputs["x"]),
        "in_w2": w2_laid.reshape(P, C * NIDX),
        "in_mlp": mlp,
        "in_bands": _bands(),
    }
    nc = bacc.Bacc("TRN2", target_bir_lowering=False, num_devices=1)
    args = [nc.dram_tensor(name, a.shape, mybir.dt.from_np(a.dtype), kind="ExternalInput").ap()
            for name, a in arrays.items()]
    args.append(nc.dram_tensor("out", (B, C, H, W), F32, kind="ExternalOutput").ap())
    build(nc, *args)
    r = run_bass_kernel_spmd(nc, [arrays], core_ids=[0])
    return r.results[0]["out"]
```

```python
from contextlib import ExitStack

import concourse.bass as bass
from concourse import mybir

F32 = mybir.dt.float32
F32R = mybir.dt.float32r
ACT = mybir.ActivationFunctionType
ALU = mybir.AluOpType
RMAX = bass.bass_isa.ReduceOp.max

P = 128
B, C, H, W, K = 16, 64, 256, 256, 7
PAD = K // 2
HALVES = H // P
PAIRS = C // 2
HID = C // 4
ROWP = W + PAD
WIDE = W + 2 * PAD
SLOTS = C * HALVES
Y_LEN = SLOTS * ROWP + 8
VLEN = 264
TAP0 = 127
NQ = 4
NIDX = 13
EPS = 1e-5
SIGMA_MIN, SIGMA_SPAN = 0.6, 0.6
SMOOTH, SMOOTH_NEG, DIFF, DIFF2, BLUR = 0, 1, 2, 3, 4
N_BANDS = 7


def build(nc, x, w2_laid, mlp_laid, bands, out):
    x_img = x.rearrange("b c (t p) w -> b c p t w", p=P)
    out_img = out.rearrange("b c (t p) w -> b c p t w", p=P)
    tap_table = nc.dram_tensor("tap_table", (C, K, VLEN), F32).ap()
    tap_main = bass.AP(tensor=tap_table.tensor, offset=PAD, ap=[[K * VLEN, C], [1, P], [VLEN, K], [1, P]])
    beyond_rows = list(range(-PAD, 0)) + list(range(P, P + PAD))
    tap_beyond = nc.dram_tensor("tap_beyond", (C, len(beyond_rows), K, P), F32).ap()
    tap_rows = [bass.AP(tensor=tap_table.tensor, offset=PAD + r, ap=[[K * VLEN, C], [VLEN, K], [1, P]])
                for r in beyond_rows]

    with ExitStack() as ctx:
        def sb(name, shape, dt=F32):
            return ctx.enter_context(nc.sbuf_tensor(name, shape, dt))

        def bank(name):
            return ctx.enter_context(nc.psum_tensor(name, [P, HALVES, W], F32))

        def sem(name):
            return ctx.enter_context(nc.semaphore(name))

        images = sb("images", [P, Y_LEN])
        x_raw = sb("x_raw", [P, 2, HALVES, WIDE])
        x_stream = sb("x_stream", [P, HALVES, W])
        x_parts = sb("x_parts", [P, HALVES, 2, 2, WIDE], F32R)
        halo = sb("halo", [P, HALVES, 2, 2, WIDE], F32R)
        hankel = sb("hankel", [P, K + 1, P])
        taps = sb("taps", [P, 2, K + 1, P], F32R)
        y_parts = sb("y_parts", [P, 2, HALVES, W + 2], F32R)
        pair_sum = sb("pair_sum", [P, PAD, HALVES, W])
        blurred = sb("blurred", [P, HALVES, W])
        b_parts = sb("b_parts", [P, 2, HALVES, W], F32R)
        result = sb("result", [P, 2, HALVES, W])
        gauss = sb("gauss", [P, PAD + 1, HALVES, W])
        edge = sb("edge", [P, HALVES, W])
        band = sb("band", [P, N_BANDS, 3, P], F32R)
        ones = sb("ones", [P, P])
        x_stats = sb("x_stats", [P, C, 6])
        x_mean = sb("x_mean", [P, PAIRS])
        x_mean_neg = sb("x_mean_neg", [P, PAIRS])
        y_mean = sb("y_mean", [P, PAIRS])
        y_std = sb("y_std", [P, PAIRS])
        minus_half = sb("minus_half", [P, PAIRS])
        x1_sums = sb("x1_sums", [P, 2, 2])
        pair_sums_x1 = sb("pair_sums_x1", [P, 2])
        dev = sb("dev", [P, 2])
        moments = sb("moments", [P, 2])
        var1 = sb("var1", [P, 3])
        rstd1 = sb("rstd1", [P, 1])
        extreme = sb("extreme", [P, 2])
        extreme_all = sb("extreme_all", [P, 2])
        scale_e = sb("scale_e", [P, 4])

        ps_conv = bank("ps_conv")
        ps_blur = [bank(f"ps_blur{k}") for k in range(PAD)]
        ps_gx = bank("ps_gx")
        ps_gy = bank("ps_gy")
        ps_small = bank("ps_small").rearrange("p t w -> p (t w)")

        const_in = sem("const_in")
        table_zeroed = sem("table_zeroed")
        stream_in = sem("stream_in")
        x_in = [sem(f"x_in{u}") for u in range(2)]
        hankel_in = [sem(f"hankel_in{j}") for j in range(2)]
        halo_in = [sem(f"halo_in{j}") for j in range(6)]
        mlp_in = sem("mlp_in")
        table_in = sem("table_in")
        beyond_in = [sem(f"beyond_in{j}") for j in range(2)]
        stored = [sem(f"stored{u}") for u in range(2)]
        cleared = sem("cleared")
        constants = sem("constants")
        bands_ready = sem("bands_ready")
        streamed = sem("streamed")
        padded = sem("padded")
        x_high = sem("x_high")
        x_low = sem("x_low")
        taps_high = sem("taps_high")
        taps_low = sem("taps_low")
        conv_done = sem("conv_done")
        x1_out = sem("x1_out")
        x1_squared = sem("x1_squared")
        chain = sem("chain")
        mean_mm = sem("mean_mm")
        moments_out = sem("moments_out")
        normed = sem("normed")
        y_high = sem("y_high")
        y_low = sem("y_low")
        sobel_mm = sem("sobel_mm")
        squared = sem("squared")
        edge_add = sem("edge_add")
        sums = sem("sums")
        hblur = sem("hblur")
        b_high = sem("b_high")
        b_low = sem("b_low")
        vblur_mm = sem("vblur_mm")
        vblur = sem("vblur")
        residual = sem("residual")
        centre = sem("centre")
        xs = sem("xs")
        xs_mm = sem("xs_mm")
        xs_act = sem("xs_act")
        xs_pow = sem("xs_pow")
        maps = sem("maps")
        maps_exp = sem("maps_exp")
        maps_all = sem("maps_all")
        edge_clear = sem("edge_clear")
        held = {e: sem(f"held_{e}") for e in ("act", "dve", "pool", "sp")}
        CHAIN, HSTEPS, VSTEPS = 9, 7, 6
        XS, XS_MM, XS_ACT, MAPS = 22, 5, 2, 18

        def need(eng, s, value):
            if not isinstance(value, int) or value > 0:
                eng.wait_ge(s, value)

        def alone(wait, engine):
            wait.then_inc(held[engine], 1)

        def slot(i, u, d=0):
            off = i * (2 * HALVES * ROWP) + (u * HALVES * ROWP + PAD + d)
            v = images[:, bass.ds(off, HALVES * ROWP)]
            return v.rearrange("p (t w) -> p t w", t=HALVES)[:, :, 0:W]

        def col(t, i):
            return t[:, bass.ds(i, 1)]

        def batches(eng, one):
            one(0, front=True, back=False, stream=True)
            with eng.Fori(1, B - 1) as k:
                one(k, front=True, back=True, stream=True)
            one(B - 1, front=True, back=True, stream=False)
            one(B, front=False, back=True, stream=False)

        def pairs(eng, k, body):
            body(k * PAIRS, 0, False, True)
            with eng.Fori(1, PAIRS - 1) as i:
                body(k * PAIRS + i, i, True, True)
            body(k * PAIRS + (PAIRS - 1), PAIRS - 1, True, False)

        mlp_in_sb = pair_sum[:, 1].rearrange("p t w -> p (t w)")
        w1_sb = mlp_in_sb[0:C, 0:P]
        b1_sb = mlp_in_sb[:, P:P + 1]
        mask_sb = mlp_in_sb[:, P + 1:P + 1 + NQ]
        b2_sb = mlp_in_sb[0:C, P + 5:P + 5 + NQ * NIDX]
        w2_sb = hankel[:, 0:K, :].rearrange("p a b -> p (a b)")[:, 0:C * NIDX].rearrange("p (c j) -> p c j", j=NIDX)
        scratch = pair_sum[:, 0].rearrange("p t w -> p (t w)")
        tmp_a, tmp_b, tmp_c, ch_mean, pooled = (scratch[:, j * C:(j + 1) * C] for j in range(5))
        gvar = scratch[:, 5 * C:5 * C + PAIRS]
        x_rstd = scratch[:, 5 * C + PAIRS:6 * C]
        small_v = scratch[:, 6 * C:6 * C + 16]
        tap_w = scratch[0:C, 7 * C:7 * C + NQ * NIDX]
        map_t = blurred
        map_u = pair_sum[:, 2]

        block = ctx.enter_context(nc.Block())

        @block.sync
        def _(sp):
            sp.dma_start(images[:, 0:N_BANDS * 3 * P], bands).then_inc(const_in, 16)
            sp.wait_ge(cleared, 4)
            sp.dma_start(tap_table.rearrange("c k v -> c (k v)"),
                         gauss.ap().rearrange("p a t w -> p (a t w)")[0:C, 0:K * VLEN]).then_inc(table_zeroed, 16)

            def load_stream(s, k, c):
                need(sp, streamed, s)
                src = x_img[bass.ds(k, 1), bass.ds(c, 1)].rearrange("a b p t w -> p (a b t) w")
                sp.dma_start(x_stream[:, :, :], src).then_inc(stream_in, 16)

            def load_x(n, k, i, u):
                need(sp, x_low, 2 * n + u - 1)
                src = x_img[bass.ds(k, 1), bass.ds(i * 2 + u, 1)].rearrange("a b p t w -> p (a b t) w")
                sp.dma_start(x_raw[:, u, :, PAD:PAD + W], src).then_inc(x_in[u], 16)

            def load_hankel(m, c):
                need(sp, taps_low, m)
                ch = bass.ds(c, 1)
                sp.dma_start(hankel[:, 0:K, :], tap_main[ch].rearrange("a p d j -> p (a d) j")
                             ).then_inc(hankel_in[0], 16)
                sp.dma_start(hankel[0:len(beyond_rows) * K, K, :], tap_beyond[ch].rearrange("a e d j -> (a e d) j")
                             ).then_inc(hankel_in[1], 16)

            def load_halo(n):
                sp.wait_ge(x_low, 2 * n + 2)
                need(sp, conv_done, 2 * n)
                j = 0
                for t in range(HALVES):
                    for e in range(2 * PAD):
                        if t == 0:
                            row, part = (PAD - e, 0) if e < PAD else (e - PAD, 1)
                        else:
                            row, part = (P - PAD + e, 0) if e < PAD else (P - 2 - (e - PAD), 1)
                        pitch, run = HALVES * 4 * WIDE, 4 * WIDE - 2 * PAD
                        src = bass.AP(tensor=x_parts, offset=row * pitch + part * 4 * WIDE,
                                      ap=[[pitch, 1], [1, K], [1, run]])
                        dst = halo[e * K:(e + 1) * K, t].rearrange("p a b w -> p (a b w)")[:, 0:run]
                        sp.dma_start(dst.bitcast(F32), src.bitcast(F32)).then_inc(halo_in[j % 6], 16)
                        j += 1

            def store(nb, k, i, u):
                sp.wait_ge(vblur, VSTEPS * (2 * nb + u + 1))
                dst = out_img[bass.ds(k, 1), bass.ds(i * 2 + u, 1)].rearrange("a b p t w -> p (a b t) w")
                sp.dma_start(dst, result[:, u]).then_inc(stored[u], 16)

            def load_mlp(k):
                if isinstance(k, int) and k == 0:
                    sp.wait_ge(cleared, 4)
                else:
                    alone(sp.wait_ge(taps_low, C * k), "sp")
                    need(sp, hblur, (k - 1) * (C * HSTEPS))
                sp.dma_start(hankel[:, 0:K, :].rearrange("p a b -> p (a b)")[:, 0:C * NIDX], w2_laid
                             ).then_inc(mlp_in, 16)
                sp.dma_start(mlp_in_sb[:, 0:P + 5 + NQ * NIDX], mlp_laid).then_inc(mlp_in, 16)

            def write_table(k):
                if isinstance(k, int) and k == 0:
                    sp.wait_ge(table_zeroed, 16)
                sp.wait_ge(xs, XS * (k + 1))
                sp.dma_start(tap_table[:, :, TAP0:TAP0 + K], tap_w[:, 0:K * K].rearrange("p (d j) -> p d j", d=K)
                             ).then_inc(table_in, 16)
                sp.wait_ge(table_in, 16 * (k + 1))
                for e, src in enumerate(tap_rows):
                    sp.dma_start(tap_beyond[:, e], src).then_inc(beyond_in[e % 2], 16)
                for s in beyond_in:
                    sp.wait_ge(s, 48 * (k + 1))

            def enter(k, last_store):
                for u in range(2):
                    load_x(k * PAIRS, k, 0, u)
                load_mlp(k)
                last_store()
                write_table(k)
                load_hankel(k * C, 0)
                load_halo(k * PAIRS)

            def batch(k, front, back, stream):
                def body(n, i, behind, ahead):
                    if front:
                        load_hankel(2 * n + 1, i * 2 + 1)
                        if ahead:
                            load_x(n + 1, k, i + 1, 0)
                            load_x(n + 1, k, i + 1, 1)
                    if back and behind:
                        store(n - 1 - PAIRS, k - 1, i - 1, 1)
                    if stream:
                        load_stream(2 * n + C, k + 1, i * 2)
                    if front and ahead:
                        load_hankel(2 * n + 2, i * 2 + 2)
                    if stream:
                        load_stream(2 * n + C + 1, k + 1, i * 2 + 1)
                    if back:
                        store(n - PAIRS, k - 1, i, 0)
                    if front and ahead:
                        load_halo(n + 1)
                pairs(sp, k, body)

                def last_store():
                    if back:
                        store((k - 1) * PAIRS + (PAIRS - 1), k - 1, PAIRS - 1, 1)
                if stream:
                    enter(k + 1, last_store)
                else:
                    last_store()

            with sp.Fori(0, C) as c:
                load_stream(c, 0, c)
            enter(0, lambda: None)
            batches(sp, batch)
            for u in range(2):
                sp.wait_ge(stored[u], 16 * B * PAIRS)

        @block.gpsimd
        def _(pool):
            def pair_sums(b, i, u, first=False):
                for d in range(1, PAD + 1):
                    if not first:
                        pool.wait_ge(hblur, (b - 1) * HSTEPS + (4, 6, 7)[d - 1])
                    pool.tensor_tensor(pair_sum[:, d - 1], slot(i, u, -d), slot(i, u, d), ALU.add).then_inc(sums, 1)

            def add_centre(b, u):
                pool.wait_ge(residual, b + 1)
                pool.wait_ge(hblur, HSTEPS * (b + 1))
                pool.tensor_tensor(result[:, u], result[:, u], blurred[:, :, :], ALU.add).then_inc(centre, 1)

            def pad_x(n, u):
                alone(pool.wait_ge(x_in[u], 16 * (n + 1)), "pool")
                pitch = 2 * HALVES * WIDE
                base = u * HALVES * WIDE
                src = bass.AP(tensor=x_raw, offset=base + 2 * PAD, ap=[[pitch, P], [WIDE, 2], [W - 5, 2], [-1, PAD]])
                dst = bass.AP(tensor=x_raw, offset=base, ap=[[pitch, P], [WIDE, 2], [W + PAD, 2], [1, PAD]])
                pool.tensor_copy(dst, src).then_inc(padded, 1)

            def split_taps(m):
                pool.wait_ge(taps_high, m + 1)
                rev = bass.AP(tensor=hankel, offset=P - 1, ap=[[(K + 1) * P, P], [P, K + 1], [-1, P]])
                pool.tensor_tensor(taps[:, 1], rev, taps[:, 0].bitcast(F32), ALU.subtract).then_inc(taps_low, 1)

            def stats_step(n, j, ins):
                ins.then_inc(chain, 1)
                wait = pool.wait_ge(chain, CHAIN * n + j)
                if j in (1, 5, CHAIN):
                    alone(wait, "pool")

            def partition_moments(n, i):
                pool.wait_ge(x1_squared, 2 * n + 2)
                need(pool, mean_mm, n)
                stats_step(n, 1, pool.tensor_tensor(pair_sums_x1[:, :], x1_sums[:, 0], x1_sums[:, 1], ALU.add))
                stats_step(n, 2, pool.tensor_scalar(dev[:, :], pair_sums_x1[:, :], 1.0 / (2 * HALVES * W), None,
                                                    ALU.mult))
                stats_step(n, 3, pool.tensor_tensor(dev[:, 0:1], dev[:, 0:1], col(x_mean, i), ALU.subtract))

            def group_moments(n, i, back):
                pool.wait_ge(moments_out, n + 1)
                stats_step(n, 4, pool.tensor_tensor(var1[:, 0:1], moments[:, 0:1], moments[:, 0:1], ALU.mult))
                stats_step(n, 5, pool.tensor_tensor(var1[:, 1:2], moments[:, 1:2], var1[:, 0:1], ALU.subtract))
                stats_step(n, 6, pool.tensor_scalar(var1[:, 2:3], var1[:, 1:2], 0.0, EPS, ALU.max, ALU.add))
                need(pool, normed, 2 * n)
                stats_step(n, 7, pool.tensor_tensor(rstd1[:, :], var1[:, 2:3], minus_half[:, 0:1], ALU.pow))
                if back:
                    pool.wait_ge(residual, 2 * n + 2 - C)
                stats_step(n, 8, pool.tensor_tensor(col(y_mean, i), moments[:, 0:1], col(x_mean, i), ALU.add))
                stats_step(n, 9, pool.tensor_tensor(col(y_std, i), var1[:, 2:3], rstd1[:, :], ALU.mult))

            def split_y(m, i, u):
                pool.wait_ge(y_high, m + 1)
                pool.tensor_tensor(y_parts[:, 1, :, 1:1 + W], slot(i, u), y_parts[:, 0, :, 1:1 + W].bitcast(F32),
                                   ALU.subtract).then_inc(y_low, 1)

            def batch(k, front, back, stream):
                if back:
                    pool.wait_ge(maps, MAPS * k)
                    if front:
                        pool.wait_ge(table_in, 16 * (k + 1))
                    pair_sums(k * C - C, 0, 0, first=True)

                def body(n, i, behind, ahead):
                    m, b = 2 * n, 2 * n - C
                    if back:
                        pair_sums(b + 1, i, 1)
                    if front and behind:
                        split_y(m - 2, i - 1, 0)
                    if back:
                        add_centre(b, 0)
                    if front:
                        if ahead:
                            pad_x(n + 1, 0)
                            pad_x(n + 1, 1)
                        split_taps(m + 1)
                    if back:
                        add_centre(b + 1, 1)
                    if front and behind:
                        split_y(m - 1, i - 1, 1)
                    if back and ahead:
                        pair_sums(b + 2, i + 1, 0)
                    if front:
                        partition_moments(n, i)
                        if ahead:
                            split_taps(m + 2)
                        group_moments(n, i, back)
                pairs(pool, k, body)
                if front:
                    split_y((k + 1) * C - 2, PAIRS - 1, 0)
                if stream:
                    enter(k + 1)
                if front:
                    split_y((k + 1) * C - 1, PAIRS - 1, 1)
                    alone(pool.wait_ge(maps, MAPS * k + 3), "pool")
                    pool.partition_all_reduce(extreme_all[:, :], extreme[:, :], P, RMAX).then_inc(maps_all, 1)
                if stream:
                    split_taps((k + 1) * C)

            def enter(k):
                pad_x(k * PAIRS, 0)
                pad_x(k * PAIRS, 1)
                x_power(k)

            def x_power(k):
                pool.wait_ge(xs, XS * k + 14)
                pool.tensor_tensor(x_rstd, gvar, minus_half[:, :], ALU.pow).then_inc(xs_pow, 1)

            pool.memset(minus_half[:, :], -0.5).then_inc(constants, 1)
            pool.memset(ones[:, :], 1.0 / P).then_inc(constants, 1)
            pool.wait_ge(constants, 2)
            enter(0)
            split_taps(0)
            batches(pool, batch)

        @block.scalar
        def _(act):
            def rebuild_x1(b, i, u):
                need(act, stored[u], (b - u) * 8)
                alone(act.wait_ge(normed, b + 1), "act")
                nc.scalar.activation(result[:, u], slot(i, u), ACT.Identity, bias=col(y_mean, i),
                                     scale=col(y_std, i)).then_inc(residual, 1)

            def round_blurred(b):
                act.wait_ge(hblur, HSTEPS * (b + 1))
                need(act, vblur_mm, 3 * b)
                nc.scalar.activation(b_parts[:, 0], blurred[:, :, :], ACT.Copy).then_inc(b_high, 1)

            def move_x1(n, i, u, back):
                m = 2 * n + u
                if back:
                    act.wait_ge(hblur, HSTEPS * (m - C + 1))
                    act.wait_ge(residual, m - C + 1)
                need(act, chain, CHAIN * n)
                alone(act.wait_ge(conv_done, m + 1), "act")
                nc.scalar.activation(slot(i, u), ps_conv[:, :, :], ACT.Identity, bias=col(x_mean, i),
                                     accum_out=x1_sums[:, u, 0:1]).then_inc(x1_out, 1)

            def square_x1(m, u):
                act.wait_ge(x1_out, m + 1)
                nc.scalar.activation(ps_conv[:, :, :], ps_conv[:, :, :], ACT.Square,
                                     accum_out=x1_sums[:, u, 1:2]).then_inc(x1_squared, 1)

            def round_taps(m):
                for s in hankel_in:
                    act.wait_ge(s, 16 * (m + 1))
                need(act, conv_done, m)
                rev = bass.AP(tensor=hankel, offset=P - 1, ap=[[(K + 1) * P, P], [P, K + 1], [-1, P]])
                nc.scalar.activation(taps[:, 0], rev, ACT.Copy).then_inc(taps_high, 1)

            def round_x(n, i, u):
                need(act, conv_done, 2 * n + u - 1)
                alone(act.wait_ge(padded, 2 * n + u + 1), "act")
                nc.scalar.activation(x_parts[:, :, u, 0], x_raw[:, u], ACT.Identity,
                                     bias=col(x_mean_neg, i)).then_inc(x_high, 1)

            def move_moments(n):
                act.wait_ge(mean_mm, n + 1)
                nc.scalar.activation(moments[:, :], ps_small[:, 0:2], ACT.Copy).then_inc(moments_out, 1)

            def round_y(m, i, u):
                need(act, sobel_mm, 2 * m)
                alone(act.wait_ge(normed, m + 1), "act")
                nc.scalar.activation(y_parts[:, 0, :, 1:1 + W], slot(i, u), ACT.Copy).then_inc(y_high, 1)

            def square(m):
                for j, g in enumerate((ps_gx, ps_gy)):
                    act.wait_ge(sobel_mm, 2 * m + j + 1)
                    nc.scalar.activation(g[:, :, :], g[:, :, :], ACT.Square).then_inc(squared, 1)

            def batch(k, front, back, stream):
                if back:
                    round_blurred(k * C - C)

                def body(n, i, behind, ahead):
                    m, b = 2 * n, 2 * n - C
                    if front and behind:
                        round_y(m - 2, i - 1, 0)
                    if back:
                        rebuild_x1(b, i, 0)
                    if front:
                        move_x1(n, i, 0, back)
                        if ahead:
                            round_x(n + 1, i + 1, 0)
                        square_x1(m, 0)
                        round_taps(m + 1)
                    if back:
                        round_blurred(b + 1)
                    if front and behind:
                        square(m - 2)
                        round_y(m - 1, i - 1, 1)
                    if back:
                        rebuild_x1(b + 1, i, 1)
                    if front:
                        if ahead:
                            round_x(n + 1, i + 1, 1)
                        move_x1(n, i, 1, back)
                        square_x1(m + 1, 1)
                        if ahead:
                            round_taps(m + 2)
                        move_moments(n)
                    if back and ahead:
                        round_blurred(b + 2)
                    if front and behind:
                        square(m - 1)
                pairs(act, k, body)
                m = (k + 1) * C - 2
                if front:
                    round_y(m, PAIRS - 1, 0)
                    square(m)
                    round_y(m + 1, PAIRS - 1, 1)
                if stream:
                    enter(k + 1)
                if front:
                    square(m + 1)
                if stream:
                    round_taps((k + 1) * C)
                if front:
                    for d in range(1, PAD + 1):
                        if d == 1:
                            act.wait_ge(maps, MAPS * k + 11)
                        nc.scalar.activation(gauss[:, d], map_u, ACT.Exp, scale=-float(d * d)).then_inc(maps_exp, 1)

            def enter(k):
                act.wait_ge(xs, XS * k + 5)
                round_x(k * PAIRS, 0, 0)
                round_x(k * PAIRS, 0, 1)
                weights(k)

            def weights(k):
                act.wait_ge(mlp_in, 32 * (k + 1))
                act.wait_ge(xs_mm, XS_MM * k + 4)
                nc.scalar.activation(small_v[:, 1:2], ps_small[:, 130:131], ACT.Gelu,
                                     bias=b1_sb).then_inc(xs_act, 1)
                act.wait_ge(xs, XS * k + 20)
                nc.scalar.activation(tap_w, tap_w, ACT.Sigmoid).then_inc(xs_act, 1)

            act.wait_ge(const_in, 16)
            nc.scalar.activation(band.ap().rearrange("p a b c -> p (a b c)"), images[:, 0:N_BANDS * 3 * P],
                                 ACT.Copy).then_inc(bands_ready, 1)
            enter(0)
            round_taps(0)
            batches(act, batch)

        @block.tensor
        def _(pe):
            def banded(ps, kind, parts, start, stop):
                last = None
                for j, part in enumerate(parts):
                    nc.tensor.matmul(ps[:, :, :], band[:, kind, 0], part, start=start and j == 0, stop=False)
                    nc.tensor.matmul(ps[:, 0], band[:, kind, 1], part[:, 1], start=False, stop=False)
                    last = nc.tensor.matmul(ps[:, 1], band[:, kind, 2], part[:, 0], start=False,
                                            stop=stop and j == len(parts) - 1)
                return last

            def convolve(n, u):
                m = 2 * n + u
                pe.wait_ge(taps_low, m + 1)
                pe.wait_ge(x_low, m + 1)
                need(pe, x1_squared, m)
                passes = ((0, 0), (1, 0), (0, 1))
                for j, (tp, xp) in enumerate(passes):
                    for d in range(K):
                        nc.tensor.matmul(ps_conv[:, :, :], taps[:, tp, d], x_parts[:, :, u, xp, d:d + W],
                                         start=(j == 0 and d == 0), stop=False)
                for s in halo_in:
                    pe.wait_ge(s, 32 * (n + 1))
                for j, (tp, xp) in enumerate(passes):
                    last = nc.tensor.matmul(ps_conv[:, :, :], taps[:, tp, K], halo[:, :, u, xp, 0:W],
                                            start=False, stop=(j == 2))
                last.then_inc(conv_done, 1)

            def vertical(b):
                pe.wait_ge(b_low, b + 1)
                need(pe, vblur, b * VSTEPS)
                for d in range(PAD):
                    banded(ps_blur[d], BLUR + d, (b_parts[:, 0], b_parts[:, 1]), True, True).then_inc(vblur_mm, 1)

            def sobel_x(m):
                pe.wait_ge(y_low, m + 1)
                part = lambda s, hl: y_parts[:, hl, :, 1 + s:1 + s + W]
                need(pe, edge_add, 2 * m)
                banded(ps_gx, SMOOTH, (part(1, 0), part(1, 1)), True, False)
                banded(ps_gx, SMOOTH_NEG, (part(-1, 0), part(-1, 1)), False, True).then_inc(sobel_mm, 1)

            def sobel_y(m):
                part = lambda s, hl: y_parts[:, hl, :, 1 + s:1 + s + W]
                banded(ps_gy, DIFF, (part(1, 0), part(1, 1), part(-1, 0), part(-1, 1)), True, False)
                banded(ps_gy, DIFF2, (part(0, 0), part(0, 1)), False, True).then_inc(sobel_mm, 1)

            def group_mean(n):
                pe.wait_ge(chain, CHAIN * n + 3)
                need(pe, moments_out, n)
                nc.tensor.matmul(ps_small[:, 0:2], ones[:, :], dev[:, :], start=True, stop=True).then_inc(mean_mm, 1)

            def batch(k, front, back, stream):
                def body(n, i, behind, ahead):
                    m, b = 2 * n, 2 * n - C
                    if front:
                        convolve(n, 0)
                    if back:
                        vertical(b)
                    if front and behind:
                        sobel_x(m - 2)
                        sobel_y(m - 2)
                    if front:
                        convolve(n, 1)
                    if back:
                        vertical(b + 1)
                    if front:
                        if behind:
                            sobel_x(m - 1)
                        group_mean(n)
                        if behind:
                            sobel_y(m - 1)
                pairs(pe, k, body)
                m = (k + 1) * C - 2
                if stream:
                    x_means(k + 1)
                if front:
                    sobel_x(m)
                if stream:
                    x_variances(k + 1)
                if front:
                    sobel_y(m)
                if stream:
                    mlp(k + 1)
                if front:
                    sobel_x(m + 1)
                    sobel_y(m + 1)

            def x_means(k):
                pe.wait_ge(xs, XS * k + 1)
                need(pe, moments_out, k * PAIRS)
                nc.tensor.matmul(ps_small[:, 0:C], ones[:, :], tmp_a, start=True, stop=True).then_inc(xs_mm, 1)

            def x_variances(k):
                pe.wait_ge(xs, XS * k + 13)
                nc.tensor.matmul(ps_small[:, C:C + PAIRS], ones[:, :], tmp_c[:, 0:PAIRS], start=True,
                                 stop=True).then_inc(xs_mm, 1)

            def mlp(k):
                pe.wait_ge(xs, XS * k + 17)
                nc.tensor.matmul(ps_small[0:C, 128:129], pooled, ones[:, 0:1], start=True, stop=True)
                nc.tensor.matmul(ps_small[0:C, 129:130], tmp_b, ones[:, 0:1], start=True,
                                 stop=True).then_inc(xs_mm, 1)
                pe.wait_ge(xs, XS * k + 18)
                pe.wait_ge(mlp_in, 32 * (k + 1))
                nc.tensor.matmul(ps_small[:, 130:131], w1_sb, small_v[0:C, 3:4], start=True,
                                 stop=True).then_inc(xs_mm, 1)
                pe.wait_ge(xs, XS * k + 19)
                for j in range(NIDX):
                    last = nc.tensor.matmul(ps_small[0:C, 192 + NQ * j:192 + NQ * (j + 1)], w2_sb[:, :, j],
                                            small_v[:, 8:8 + NQ], start=True, stop=True)
                last.then_inc(xs_mm, 1)

            pe.wait_ge(bands_ready, 1)
            pe.wait_ge(constants, 2)
            pe.wait_ge(cleared, 5)
            x_means(0)
            x_variances(0)
            mlp(0)
            batches(pe, batch)

        @block.vector
        def _(dve):
            flat = lambda t: t.rearrange("p t w -> p (t w)")

            def horizontal(b, i, u):
                h = HSTEPS * b

                def product(d):
                    dve.wait_ge(sums, 3 * b + d)
                    nc.vector.tensor_tensor(pair_sum[:, d - 1], pair_sum[:, d - 1], gauss[:, d],
                                            ALU.mult).then_inc(hblur, 1)

                def add(d, done):
                    dve.wait_ge(hblur, h + done)
                    nc.vector.tensor_tensor(blurred[:, :, :], blurred[:, :, :], pair_sum[:, d - 1],
                                            ALU.add).then_inc(hblur, 1)
                product(1)
                product(2)
                need(dve, centre, b)
                need(dve, b_low, b)
                nc.vector.tensor_tensor(blurred[:, :, :], gauss[:, 0], slot(i, u), ALU.mult).then_inc(hblur, 1)
                add(1, 3)
                product(3)
                add(2, 4)
                add(3, 6)

            def split_blurred(b):
                dve.wait_ge(b_high, b + 1)
                nc.vector.tensor_tensor(b_parts[:, 1], blurred[:, :, :], b_parts[:, 0].bitcast(F32),
                                        ALU.subtract).then_inc(b_low, 1)

            def vertical(b, u):
                v = VSTEPS * b

                def product(d):
                    dve.wait_ge(vblur_mm, 3 * b + d)
                    nc.vector.tensor_tensor(ps_blur[d - 1][:, :, :], ps_blur[d - 1][:, :, :], gauss[:, d],
                                            ALU.mult).then_inc(vblur, 1)

                def add(d, done):
                    dve.wait_ge(vblur, v + done)
                    nc.vector.tensor_tensor(result[:, u], ps_blur[d - 1][:, :, :], result[:, u],
                                            ALU.add).then_inc(vblur, 1)
                product(1)
                product(2)
                dve.wait_ge(centre, b + 1)
                add(1, 1)
                product(3)
                add(2, 3)
                add(3, 5)

            def split_x(n, i, u):
                dve.wait_ge(x_high, 2 * n + u + 1)
                nc.vector.scalar_tensor_tensor(
                    out=x_parts[:, :, u, 1], in0=x_raw[:, u], scalar=col(x_mean, i),
                    in1=x_parts[:, :, u, 0].bitcast(F32),
                    op0=ALU.subtract, op1=ALU.subtract).then_inc(x_low, 1)

            def measure_stream(s, c):
                alone(dve.wait_ge(stream_in, 16 * (s + 1)), "dve")
                nc.vector.bn_stats(x_stats[:, bass.ds(c, 1), :].rearrange("p a s -> p (a s)"), flat(x_stream[:, :, :])
                                   ).then_inc(streamed, 1)

            def norm(n, i, u):
                if u == 0:
                    dve.wait_ge(chain, CHAIN * n + CHAIN)
                nc.vector.tensor_scalar(slot(i, u), slot(i, u), col(y_mean, i), rstd1[:, :], ALU.subtract,
                                        ALU.mult).then_inc(normed, 1)

            def add_edges(m):
                for j, g in enumerate((ps_gx, ps_gy)):
                    dve.wait_ge(squared, 2 * m + j + 1)
                    need(dve, edge_add, 2 * m + j)
                    nc.vector.tensor_tensor(edge[:, :, :], g[:, :, :], edge[:, :, :], ALU.add).then_inc(edge_add, 1)

            def batch(k, front, back, stream):
                if front:
                    nc.vector.memset(edge[:, :, :], 0.0).then_inc(edge_clear, 1)
                    dve.wait_ge(edge_clear, k + 1)
                if back:
                    horizontal(k * C - C, 0, 0)
                    split_blurred(k * C - C)

                def body(n, i, behind, ahead):
                    m, b = 2 * n, 2 * n - C
                    if back:
                        horizontal(b + 1, i, 1)
                    if front:
                        if ahead:
                            split_x(n + 1, i + 1, 0)
                    if back:
                        split_blurred(b + 1)
                    if stream:
                        measure_stream(m + C, i * 2)
                    if back:
                        vertical(b, 0)
                    if front and behind:
                        add_edges(m - 2)
                    if stream:
                        measure_stream(m + C + 1, i * 2 + 1)
                    if front:
                        if ahead:
                            split_x(n + 1, i + 1, 1)
                    if back and ahead:
                        horizontal(b + 2, i + 1, 0)
                    if back:
                        vertical(b + 1, 1)
                        if ahead:
                            split_blurred(b + 2)
                    if front:
                        norm(n, i, 0)
                        norm(n, i, 1)
                    if front and behind:
                        add_edges(m - 1)
                pairs(dve, k, body)
                if stream:
                    statistics(k + 1, XS * (k + 1))
                if front:
                    add_edges((k + 1) * C - 2)
                if stream:
                    enter(k + 1, XS * (k + 1))
                if front:
                    add_edges((k + 1) * C - 1)
                    weights_map(k)

            def enter(k, x):
                hidden_input(k, x)
                hidden_output(k, x)
                split_x(k * PAIRS, 0, 0)
                split_x(k * PAIRS, 0, 1)
                scale_taps(k, x)

            def weights_map(k):
                mp = MAPS * k
                dve.wait_ge(edge_add, 2 * C * (k + 1))
                nc.vector.tensor_reduce(extreme[:, 0:1], flat(edge[:, :, :]), mybir.AxisListType.X,
                                        ALU.max).then_inc(maps, 1)
                nc.vector.tensor_reduce(extreme[:, 1:2], flat(edge[:, :, :]), mybir.AxisListType.X,
                                        ALU.min).then_inc(maps, 1)
                dve.wait_ge(maps, mp + 2)
                nc.vector.tensor_scalar(extreme[:, 1:2], extreme[:, 1:2], -1.0, None, ALU.mult).then_inc(maps, 1)
                dve.wait_ge(maps_all, k + 1)
                nc.vector.tensor_scalar(scale_e[:, 0:1], extreme_all[:, 0:1], 1.0 / C, 1e-6, ALU.mult,
                                        ALU.add).then_inc(maps, 1)
                nc.vector.tensor_scalar(scale_e[:, 1:2], extreme_all[:, 1:2], 1.0 / C, None,
                                        ALU.mult).then_inc(maps, 1)
                dve.wait_ge(maps, mp + 4)
                nc.vector.reciprocal(scale_e[:, 2:3], scale_e[:, 0:1]).then_inc(maps, 1)
                dve.wait_ge(maps, mp + 6)
                need(dve, centre, k * C)
                nc.vector.tensor_scalar(map_t[:, :, :], edge[:, :, :], 1.0 / C, scale_e[:, 1:2], ALU.mult,
                                        ALU.add).then_inc(maps, 1)
                dve.wait_ge(maps, mp + 7)
                nc.vector.tensor_scalar(map_t[:, :, :], map_t[:, :, :], scale_e[:, 2:3], SIGMA_SPAN, ALU.mult,
                                        ALU.mult).then_inc(maps, 1)
                dve.wait_ge(maps, mp + 8)
                nc.vector.tensor_scalar(map_u, map_t[:, :, :], SIGMA_MIN, None, ALU.add).then_inc(maps, 1)
                dve.wait_ge(maps, mp + 9)
                nc.vector.scalar_tensor_tensor(out=map_t[:, :, :], in0=map_u, scalar=2.0, in1=map_u,
                                               op0=ALU.mult, op1=ALU.mult).then_inc(maps, 1)
                dve.wait_ge(maps, mp + 10)
                nc.vector.reciprocal(map_u, map_t[:, :, :]).then_inc(maps, 1)
                dve.wait_ge(maps_exp, 3 * (k + 1))
                nc.vector.tensor_tensor(map_t[:, :, :], gauss[:, 1], gauss[:, 2], ALU.add).then_inc(maps, 1)
                dve.wait_ge(maps, mp + 12)
                nc.vector.tensor_tensor(map_t[:, :, :], map_t[:, :, :], gauss[:, 3], ALU.add).then_inc(maps, 1)
                dve.wait_ge(maps, mp + 13)
                nc.vector.tensor_scalar(map_t[:, :, :], map_t[:, :, :], 2.0, 1.0, ALU.mult,
                                        ALU.add).then_inc(maps, 1)
                dve.wait_ge(maps, mp + 14)
                nc.vector.reciprocal(gauss[:, 0], map_t[:, :, :]).then_inc(maps, 1)
                dve.wait_ge(maps, mp + 15)
                for d in range(1, PAD + 1):
                    nc.vector.tensor_tensor(gauss[:, d], gauss[:, d], gauss[:, 0], ALU.mult).then_inc(maps, 1)
                dve.wait_ge(maps, mp + MAPS)

            def of_pair(t, u):
                return t.rearrange("p (g u) -> p u g", u=2)[:, u]

            def to_channels(t):
                return t.unsqueeze(2).broadcast_to([P, PAIRS, 2])

            def statistics(k, x):
                mean_e, mean_o, m2_e, m2_o = (x_stats[:, :, j] for j in (1, 4, 2, 5))
                groups = lambda t: t.rearrange("p (g u) -> p g u", u=2)
                dve.wait_ge(streamed, C * (k + 1))
                need(dve, hblur, (k - 1) * (C * HSTEPS))
                nc.vector.tensor_tensor(tmp_a, mean_e, mean_o, ALU.add).then_inc(xs, 1)
                dve.wait_ge(xs_mm, XS_MM * k + 1)
                nc.vector.tensor_scalar(ch_mean, ps_small[:, 0:C], 0.5, None, ALU.mult).then_inc(xs, 1)
                dve.wait_ge(xs, x + 2)
                nc.vector.tensor_tensor(tmp_b[:, 0:PAIRS], of_pair(ch_mean, 0), of_pair(ch_mean, 1),
                                        ALU.add).then_inc(xs, 1)
                dve.wait_ge(xs, x + 3)
                need(dve, chain, CHAIN * PAIRS * k)
                nc.vector.tensor_scalar(x_mean[:, :], tmp_b[:, 0:PAIRS], 0.5, None, ALU.mult).then_inc(xs, 1)
                nc.vector.tensor_scalar(x_mean_neg[:, :], tmp_b[:, 0:PAIRS], -0.5, None, ALU.mult).then_inc(xs, 1)
                dve.wait_ge(xs, x + 5)
                mean_b = to_channels(x_mean[:, :])
                nc.vector.tensor_tensor(groups(tmp_a), groups(mean_e), mean_b, ALU.subtract).then_inc(xs, 1)
                nc.vector.tensor_tensor(groups(tmp_b), groups(mean_o), mean_b, ALU.subtract).then_inc(xs, 1)
                dve.wait_ge(xs, x + 7)
                nc.vector.tensor_tensor(tmp_a, tmp_a, tmp_a, ALU.mult).then_inc(xs, 1)
                nc.vector.tensor_tensor(tmp_b, tmp_b, tmp_b, ALU.mult).then_inc(xs, 1)
                dve.wait_ge(xs, x + 9)
                nc.vector.tensor_tensor(tmp_a, tmp_a, tmp_b, ALU.add).then_inc(xs, 1)
                dve.wait_ge(xs, x + 10)
                nc.vector.tensor_tensor(tmp_b, m2_e, m2_o, ALU.add).then_inc(xs, 1)
                dve.wait_ge(xs, x + 11)
                nc.vector.scalar_tensor_tensor(out=tmp_a, in0=tmp_b, scalar=1.0 / W, in1=tmp_a, op0=ALU.mult,
                                               op1=ALU.add).then_inc(xs, 1)
                dve.wait_ge(xs, x + 12)
                nc.vector.tensor_tensor(tmp_c[:, 0:PAIRS], of_pair(tmp_a, 0), of_pair(tmp_a, 1),
                                        ALU.add).then_inc(xs, 1)
                dve.wait_ge(xs_mm, XS_MM * k + 2)
                nc.vector.tensor_scalar(gvar, ps_small[:, C:C + PAIRS], 0.25, EPS, ALU.mult,
                                        ALU.add).then_inc(xs, 1)
                nc.vector.tensor_tensor(groups(pooled), groups(ch_mean), mean_b, ALU.subtract).then_inc(xs, 1)
                dve.wait_ge(xs, x + 15)
                dve.wait_ge(xs_pow, k + 1)
                rstd_b = to_channels(x_rstd)
                nc.vector.tensor_tensor(groups(pooled), groups(pooled), rstd_b, ALU.mult).then_inc(xs, 1)
                nc.vector.tensor_copy(groups(tmp_b), rstd_b).then_inc(xs, 1)

            def hidden_input(k, x):
                dve.wait_ge(xs_mm, XS_MM * k + 3)
                nc.vector.tensor_copy(small_v[0:C, 3:5], ps_small[0:C, 128:130]).then_inc(xs, 1)

            def hidden_output(k, x):
                dve.wait_ge(xs_act, XS_ACT * k + 1)
                nc.vector.tensor_scalar(small_v[:, 8:8 + NQ], mask_sb, small_v[:, 1:2], None,
                                        ALU.mult).then_inc(xs, 1)

            def scale_taps(k, x):
                dve.wait_ge(xs_mm, XS_MM * k + 5)
                nc.vector.tensor_tensor(tap_w, ps_small[0:C, 192:192 + NQ * NIDX], b2_sb, ALU.add).then_inc(xs, 1)
                dve.wait_ge(xs_act, XS_ACT * k + 2)
                nc.vector.tensor_scalar(tap_w, tap_w, small_v[0:C, 4:5], None, ALU.mult).then_inc(xs, 1)
                dve.wait_ge(xs, x + 21)
                mid = PAD * K + PAD
                nc.vector.tensor_scalar(tap_w[:, mid:mid + 1], tap_w[:, mid:mid + 1], 1.0, None,
                                        ALU.add).then_inc(xs, 1)

            nc.vector.memset(gauss[:, :, :, :], 0.0).then_inc(cleared, 1)
            nc.vector.memset(hankel[:, :, :], 0.0).then_inc(cleared, 1)
            nc.vector.memset(halo[:, :, :, :, :].bitcast(F32), 0.0).then_inc(cleared, 1)
            nc.vector.memset(y_parts[:, :, :, :].bitcast(F32), 0.0).then_inc(cleared, 1)
            dve.wait_ge(bands_ready, 1)
            pads = images[:, 0:SLOTS * ROWP].rearrange("p (r w) -> p r w", w=ROWP)
            nc.vector.memset(pads[:, :, 0:PAD], 0.0)
            nc.vector.memset(images[:, SLOTS * ROWP:Y_LEN], 0.0).then_inc(cleared, 1)
            with dve.Fori(0, C) as c:
                measure_stream(c, c)
            dve.wait_ge(cleared, 5)
            statistics(0, 0)
            enter(0, 0)
            batches(dve, batch)


def _bands():
    import numpy as np
    rows = np.arange(P)[:, None]
    cols = np.arange(P)[None, :]
    out = np.zeros((P, N_BANDS, 3, P), np.float32)
    for part, dist in enumerate((rows - cols, P + rows - cols, rows - cols - P)):
        smooth = 2.0 * (dist == 0) + (abs(dist) == 1)
        diff = 1.0 * (dist == 1) - (dist == -1)
        kinds = [smooth, -smooth, diff, 2 * diff]
        kinds += [1.0 * (abs(dist) == d) - 2.0 * (dist == 0) for d in range(1, PAD + 1)]
        for kind, m in enumerate(kinds):
            out[:, kind, part] = m
    return out.reshape(P, -1)


def kernel(**inputs):
    import numpy as np
    import concourse.bacc as bacc
    from concourse.bass_utils import run_bass_kernel_spmd

    w1, b1 = np.asarray(inputs["L0_conv_w1"]), np.asarray(inputs["L0_conv_b1"])
    w2, b2 = np.asarray(inputs["L0_conv_w2"]), np.asarray(inputs["L0_conv_b2"])
    w2_taps = w2.reshape(HID, C, K, K).transpose(0, 1, 3, 2).reshape(HID, C, K * K)
    w2_full = np.zeros((HID, C, NQ * NIDX), np.float32)
    w2_full[:, :, :K * K] = w2_taps
    w2_laid = np.zeros((NQ, P // NQ, C, NIDX), np.float32)
    w2_laid[:, :HID] = w2_full.reshape(HID, C, NIDX, NQ).transpose(3, 0, 1, 2)
    mlp = np.zeros((P, P + 5 + NQ * NIDX), np.float32)
    for q in range(NQ):
        at = q * (P // NQ)
        mlp[0:C, at:at + HID] = w1
        mlp[at:at + HID, P] = b1
        mlp[at:at + HID, P + 1 + q] = 1.0
    mlp[0:C, P + 5:P + 5 + K * K] = b2.reshape(C, K, K).transpose(0, 2, 1).reshape(C, K * K)

    arrays = {
        "in_x": np.ascontiguousarray(inputs["x"]),
        "in_w2": w2_laid.reshape(P, C * NIDX),
        "in_mlp": mlp,
        "in_bands": _bands(),
    }
    nc = bacc.Bacc("TRN2", target_bir_lowering=False, num_devices=1)
    args = [nc.dram_tensor(name, a.shape, mybir.dt.from_np(a.dtype), kind="ExternalInput").ap()
            for name, a in arrays.items()]
    args.append(nc.dram_tensor("out", (B, C, H, W), F32, kind="ExternalOutput").ap())
    build(nc, *args)
    r = run_bass_kernel_spmd(nc, [arrays], core_ids=[0])
    return r.results[0]["out"]
```
